# Optimizing a Trainium2 kernel written in Bass

```python
import numpy as np
import jax
import jax.numpy as jnp

def _softmax(x, axis=-1):
    return jax.nn.softmax(x, axis=axis)

def _gelu(x):
    return jax.nn.gelu(x, approximate=True)

def _silu(x):
    return jax.nn.silu(x)

def _sigmoid(x):
    return jax.nn.sigmoid(x)

def _layernorm(x, axis=-1, eps=1e-05):
    m = jnp.mean(x, axis=axis, keepdims=True)
    v = jnp.var(x, axis=axis, keepdims=True)
    return (x - m) / jnp.sqrt(v + eps)

def _scatter_add(tgt, idx, src, axis=0):
    return tgt.at[idx].add(src)

def _segment_sum(src, seg, n):
    return jax.ops.segment_sum(src, seg, n)
kernel_name = 'mk_seq_preln_d1_jaxref_r8_4cb5c0'

def setup_inputs(seed: int=0):
    np.random.seed(seed)
    _w = jnp.asarray

    def _L0_attn_setup():
        import jax, jax.numpy as jnp
        import numpy as np
        HEADS = 16
        DIM_HEAD = 64
        EPS = 1e-08
        key = jax.random.key(seed)
        ks = jax.random.split(key, 5)
        B, N, D = (2, 256, 128)
        inner = HEADS * DIM_HEAD
        return {'x': jax.random.normal(ks[0], (B, N, D), jnp.float32), 'Wq': jax.random.normal(ks[1], (D, inner), jnp.float32) * D ** (-0.5), 'Wkv': jax.random.normal(ks[2], (D, 2 * inner), jnp.float32) * D ** (-0.5), 'Wo': jax.random.normal(ks[3], (inner, D), jnp.float32) * inner ** (-0.5), 'bo': jax.random.normal(ks[4], (D,), jnp.float32) * 0.02}
    _L0_attn_in = _L0_attn_setup()

    def _L0_ffn_setup():
        import jax, jax.numpy as jnp
        import numpy as np
        E, H, I = (8, 128, 64)
        NG, TKG, TOPK = (4, 2, 4)
        SCALE = 2.5

        def _mlp(x, wg, wu, wd):
            return jax.nn.silu(x @ wg) * (x @ wu) @ wd
        key = jax.random.key(seed)
        ks = jax.random.split(key, 8)
        s = 0.02
        return {'hidden_states': jax.random.normal(ks[0], (32, 32, H), jnp.float32), 'gate_w': jax.random.normal(ks[1], (E, H), jnp.float32) * np.float32(np.sqrt(2.0 / H)), 'correction_bias': jnp.zeros((E,), jnp.float32), 'Wg': jax.random.normal(ks[2], (E, H, I), jnp.float32) * s, 'Wu': jax.random.normal(ks[3], (E, H, I), jnp.float32) * s, 'Wd': jax.random.normal(ks[4], (E, I, H), jnp.float32) * s, 'Wg_s': jax.random.normal(ks[5], (H, I), jnp.float32) * s, 'Wu_s': jax.random.normal(ks[6], (H, I), jnp.float32) * s, 'Wd_s': jax.random.normal(ks[7], (I, H), jnp.float32) * s}
    _L0_ffn_in = _L0_ffn_setup()
    _d = {'L0_attn_x': _L0_attn_in['x'], 'L0_attn_Wq': _L0_attn_in['Wq'], 'L0_attn_Wkv': _L0_attn_in['Wkv'], 'L0_attn_Wo': _L0_attn_in['Wo'], 'L0_attn_bo': _L0_attn_in['bo'], 'L0_ffn_gate_w': _L0_ffn_in['gate_w'], 'L0_ffn_correction_bias': _L0_ffn_in['correction_bias'], 'L0_ffn_Wg': _L0_ffn_in['Wg'], 'L0_ffn_Wu': _L0_ffn_in['Wu'], 'L0_ffn_Wd': _L0_ffn_in['Wd'], 'L0_ffn_Wg_s': _L0_ffn_in['Wg_s'], 'L0_ffn_Wu_s': _L0_ffn_in['Wu_s'], 'L0_ffn_Wd_s': _L0_ffn_in['Wd_s']}
    _x0 = _d['L0_attn_x']
    _d['L0_attn_x'] = jax.random.normal(jax.random.fold_in(jax.random.key(seed), 1), (4, 1024, 128), dtype=_x0.dtype)
    del _x0
    return _d

def reference(L0_attn_x, L0_attn_Wq, L0_attn_Wkv, L0_attn_Wo, L0_attn_bo, L0_ffn_gate_w, L0_ffn_correction_bias, L0_ffn_Wg, L0_ffn_Wu, L0_ffn_Wd, L0_ffn_Wg_s, L0_ffn_Wu_s, L0_ffn_Wd_s):

    def _L0_attn_ref(x, Wq, Wkv, Wo, bo):
        import jax, jax.numpy as jnp
        import numpy as np
        HEADS = 16
        DIM_HEAD = 64
        EPS = 1e-08
        B, N, D = x.shape
        H, Dh = (HEADS, DIM_HEAD)
        scale = Dh ** (-0.5)
        q = (x @ Wq).reshape(B, N, H, Dh).transpose(0, 2, 1, 3)
        kv = x @ Wkv
        k = kv[..., :H * Dh].reshape(B, N, H, Dh).transpose(0, 2, 1, 3)
        v = kv[..., H * Dh:].reshape(B, N, H, Dh).transpose(0, 2, 1, 3)
        s = jnp.einsum('bhid,bhjd->bhij', q * scale, k)
        gm = jax.lax.stop_gradient(jnp.max(s, axis=-1, keepdims=True))
        causal_mask = jnp.triu(jnp.ones((N, N), bool), 1)
        p = jnp.where(causal_mask, 0.0, jnp.exp(s - gm))
        num = jnp.einsum('bhij,bhjd->bhid', p, v)
        out = num / (jnp.sum(p, axis=-1, keepdims=True) + EPS)
        out = out.transpose(0, 2, 1, 3).reshape(B, N, H * Dh)
        return out @ Wo + bo

    def _L0_ffn_ref(hidden_states, gate_w, correction_bias, Wg, Wu, Wd, Wg_s, Wu_s, Wd_s):
        import jax, jax.numpy as jnp
        import numpy as np
        E, H, I = (8, 128, 64)
        NG, TKG, TOPK = (4, 2, 4)
        SCALE = 2.5

        def _mlp(x, wg, wu, wd):
            return jax.nn.silu(x @ wg) * (x @ wu) @ wd
        B, T, _ = hidden_states.shape
        x = hidden_states.reshape(-1, H)
        N = x.shape[0]
        logits = x @ gate_w.T
        scores = jax.nn.sigmoid(logits)
        scores_c = scores + correction_bias
        grp = scores_c.reshape(N, NG, E // NG)
        group_scores = jnp.sum(jax.lax.top_k(grp, 2)[0], axis=-1)
        grp_idx = jax.lax.top_k(group_scores, TKG)[1]
        group_mask = jnp.zeros_like(group_scores).at[jnp.arange(N)[:, None], grp_idx].set(1.0)
        score_mask = jnp.repeat(group_mask, E // NG, axis=-1) > 0.5
        scores_for_choice = jnp.where(score_mask, scores_c, 0.0)
        topk_idx = jax.lax.top_k(scores_for_choice, TOPK)[1]
        topk_w = jnp.take_along_axis(scores, topk_idx, axis=-1)
        topk_w = topk_w / (jnp.sum(topk_w, axis=-1, keepdims=True) + 1e-20)
        topk_w = topk_w * SCALE
        cw = jnp.sum(jax.nn.one_hot(topk_idx, E, dtype=topk_w.dtype) * topk_w[..., None], axis=1)
        g = jnp.einsum('nh,ehi->eni', x, Wg)
        u = jnp.einsum('nh,ehi->eni', x, Wu)
        y = jnp.einsum('eni,eih->enh', jax.nn.silu(g) * u, Wd)
        routed = jnp.einsum('enh,ne->nh', y, cw)
        out = routed + _mlp(x, Wg_s, Wu_s, Wd_s)
        return out.reshape(B, T, H)
    x = L0_attn_x
    x = x + _L0_attn_ref(_layernorm(x, axis=-1), L0_attn_Wq, L0_attn_Wkv, L0_attn_Wo, L0_attn_bo)
    x = x + _L0_ffn_ref(_layernorm(x, axis=-1), L0_ffn_gate_w, L0_ffn_correction_bias, L0_ffn_Wg, L0_ffn_Wu, L0_ffn_Wd, L0_ffn_Wg_s, L0_ffn_Wu_s, L0_ffn_Wd_s)
    return x

_drawn_inputs = setup_inputs


def setup_inputs(seed=0):
    import zlib

    import numpy as np

    out = dict(_drawn_inputs(seed))
    spreads = {'L0_ffn_correction_bias': (0.0, 0.8)}
    factors = {'L0_attn_bo': 2.799,
     'L0_ffn_gate_w': 8.0,
     'L0_ffn_Wg': 8.0,
     'L0_ffn_Wu': 8.0,
     'L0_ffn_Wd': 8.0,
     'L0_ffn_Wg_s': 8.0,
     'L0_ffn_Wu_s': 8.0,
     'L0_ffn_Wd_s': 8.0}
    for name, (base, spread) in spreads.items():
        noise = np.random.default_rng([zlib.crc32(name.encode()), seed]).standard_normal(out[name].shape)
        drawn = base * np.exp(spread * noise) if base else spread * noise
        out[name] = jnp.asarray(drawn.astype(out[name].dtype))
    for name, factor in factors.items():
        out[name] = (out[name] * factor).astype(out[name].dtype)
    return out
```

```python
from contextlib import ExitStack

import concourse.bass as bass
from concourse import mybir
from concourse.alu_op_type import AluOpType as ALU

F32 = mybir.dt.float32
F32R = mybir.dt.float32r
ACT = mybir.ActivationFunctionType
AX = mybir.AxisListType

P = 128
BANK = 512
LN_EPS = 1e-5
DEN_EPS = 1e-8
TOPK_EPS = 1e-20
ROUTED_SCALE = 2.5
TOPK, TOP_GROUPS = 4, 2

STEPS = 16
P_SLOTS = 8
PT_SLOTS = 4
LAG_T = 5
LAG_COPY = 4
LAG_PV = 7
LAG_DOWN = 2
SHARED = {1: ("project", 0), 2: ("q", 0), 4: ("q", 1), 6: ("k", 0), 8: ("k", 1),
          10: ("project", 1), 12: ("v", 0), 14: ("v", 1)}
FILL = {("q", 0): 0, ("q", 1): 1, ("k", 0): 2, ("k", 1): 3, ("v", 0): 4, ("v", 1): 5}
FILLS = len(FILL)
SPLITS = 4


def groups_before(step):
    return sum(1 if s // 2 < 4 else 2 for s in range(step))


GROUPS = groups_before(STEPS)


def at_least(eng, sem, value):
    if isinstance(value, int) and value <= 0:
        return
    eng.wait_ge(sem, value)


def build(nc, x, Wq, Wkv, Wo, bo, gate_wT, bias, Wg, Wu, Wd, Wg_s, Wu_s, Wd_s, out):
    B, N, D = x.shape
    INNER = Wq.shape[1]
    DH = 64
    HP = INNER // P
    PAIRS = B * HP
    TB = N // P
    TILES = B * TB
    E, _, I = Wg.shape
    EI = E * I
    KD = EI // P
    NG = 4
    GS = E // NG
    QSCALE = float(DH) ** -0.5
    HALF = N // 2
    GT = HALF // P
    assert D == P and N == 2 * BANK and STEPS == 2 * TB and EI == BANK and HP == 8

    x_t = x.rearrange("b (t p) d -> p (b t) d", p=P)
    out_t = out.rearrange("b (t p) d -> p (b t) d", p=P)
    STACK_DMAS = 12
    Wo_t = Wo.rearrange("(k p) d -> p k d", p=P)
    Wd_t = Wd.rearrange("e i h -> (e i) h").rearrange("(k p) h -> p k h", p=P)

    ctx = ExitStack()
    with ctx:
        def sb(name, shape, dt=F32):
            return ctx.enter_context(nc.sbuf_tensor(name, shape, dt))

        def pb(name, shape):
            return ctx.enter_context(nc.psum_tensor(name, shape, F32))

        def sem(name):
            return ctx.enter_context(nc.semaphore(name))

        ident = sb("ident", [P, P])
        causal = sb("causal", [P, P])
        earlier = sb("earlier", [P, E, E])
        bo_all = sb("bo_all", [P, D])
        bias_all = sb("bias_all", [P, E])
        wo = sb("wo", [P, HP, D])
        wgate = sb("wgate", [P, E])
        wg = sb("wg", [P, EI])
        wu = sb("wu", [P, EI])
        wshared = sb("wshared", [P, 2 * I])
        wd = sb("wd", [P, KD + 1, D])

        stream = sb("stream", [P, TILES, D])
        xT = sb("xT", [P, B * N])
        stats = sb("stats", [P, TILES, 6])
        mean2 = sb("mean2", [P, TILES])
        mean = sb("mean", [P, TILES])
        diff = sb("diff", [P, TILES])
        var = sb("var", [P, TILES])
        m2 = sb("m2", [P, TILES])
        std = sb("std", [P, TILES])
        rstd = sb("rstd", [P, TILES])

        xcur = [sb(f"xcur{i}", [P, N]) for i in range(2)]
        wcur = [sb(f"wcur{i}", [P, 3, P]) for i in range(2)]
        q_high, q_low = sb("q_high", [P, N], F32R), sb("q_low", [P, N], F32R)
        k_high, k_low = sb("k_high", [P, N], F32R), sb("k_low", [P, N], F32R)
        q_stack = [sb(f"q_stack{i}", [P, 2, N], F32R) for i in range(2)]
        kh_stack = [sb(f"kh_stack{i}", [P, 2, N], F32R) for i in range(2)]
        kl_stack = [sb(f"kl_stack{i}", [P, 2, N], F32R) for i in range(2)]
        v = [sb(f"v{i}", [P, TB, P]) for i in range(2)]
        probs = [sb(f"probs{i}", [P, N]) for i in range(P_SLOTS)]
        probsT = [sb(f"probsT{i}", [P, N]) for i in range(PT_SLOTS)]
        heads = [sb(f"heads{i}", [P, N]) for i in range(2)]
        normed = probs[7][:].rearrange("p (t d) -> p t d", d=D)
        neg_max = sb("neg_max", [P, STEPS])
        den_left = sb("den_left", [P, STEPS])
        den_diag = sb("den_diag", [P, STEPS])
        den = sb("den", [P, STEPS])
        rden = sb("rden", [P, STEPS])

        ffn_in = [probsT[i][:, 0:GT * D].rearrange("p (t d) -> p t d", d=D) for i in range(2)]
        ffn_T = [probsT[2 + i][:, 0:GT * P] for i in range(2)]
        sig = [probs[i][:, 0:EI + I] for i in range(2)]
        act = [probs[2 + i][:, 0:EI + I] for i in range(2)]
        actT = [probs[4 + i][:, 0:(KD + 1) * P] for i in range(2)]
        result = [xcur[i][:, 0:GT * D] for i in range(2)]
        scores = [sb(f"scores{i}", [P, GT, E]) for i in range(2)]
        biased = sb("biased", [P, GT, E])
        group_score = sb("group_score", [P, GT, NG])
        tie_g, above_g = sb("tie_g", [P, GT, NG, NG]), sb("above_g", [P, GT, NG, NG])
        rank_g, keep_g = sb("rank_g", [P, GT, NG]), sb("keep_g", [P, GT, NG])
        choice = sb("choice", [P, GT, E])
        tie_e, above_e = sb("tie_e", [P, GT, E, E]), sb("above_e", [P, GT, E, E])
        rank_e, keep_e = sb("rank_e", [P, GT, E]), sb("keep_e", [P, GT, E])
        picked = sb("picked", [P, GT, E])
        total = sb("total", [P, GT])
        rtotal = sb("rtotal", [P, GT])
        weight = [sb(f"weight{i}", [P, GT, E]) for i in range(2)]

        s_ps = [pb(f"s_ps{i}", [P, N]) for i in range(2)]
        t_ps = [pb(f"t_ps{i}", [P, BANK]) for i in range(2)]
        o_ps = pb("o_ps", [P, BANK])
        m_ps = pb("m_ps", [P, BANK])

        sh_ps = [o_ps, m_ps]

        x_loaded = [sem(f"x_loaded{b}") for b in range(B)]
        w_loaded = sem("w_loaded")
        consts_set = sem("consts_set")
        consts_done = sem("consts_done")
        bo_added = sem("bo_added")
        stat_link = sem("stat_link")
        var_ready = sem("var_ready")
        std_ready = sem("std_ready")
        normed_ready = sem("normed_ready")
        normed_T = sem("normed_T")
        xT_ready = sem("xT_ready")

        pair_loaded = [sem(f"pair_loaded{i}") for i in range(2)]
        filled = sem("filled")
        act_took = sem("act_took")
        low_ready = sem("low_ready")
        stacked = sem("stacked")
        s_ready = sem("s_ready")
        max_ready = sem("max_ready")
        exp_done = sem("exp_done")
        diag_done = sem("diag_done")
        den_summed = sem("den_summed")
        rden_ready = sem("rden_ready")
        scaled = sem("scaled")
        t_ready = sem("t_ready")
        t_taken = sem("t_taken")
        pv_done = sem("pv_done")
        o_taken = sem("o_taken")
        projected = sem("projected")
        added = sem("added")

        f_normed = sem("f_normed")
        f_T = sem("f_T")
        f_T_taken = sem("f_T_taken")
        f_logits = sem("f_logits")
        f_scores = sem("f_scores")
        g_link = sem("g_link")
        f_rtotal = sem("f_rtotal")
        f_weight = sem("f_weight")
        f_up = sem("f_up")
        f_sig = sem("f_sig")
        f_sigw = sem("f_sigw")
        f_silu = sem("f_silu")
        f_act = sem("f_act")
        f_actT = sem("f_actT")
        f_actT_taken = sem("f_actT_taken")
        f_down = sem("f_down")
        f_result = sem("f_result")
        stored = [sem(f"stored{i}") for i in range(2)]

        block = ctx.enter_context(nc.Block())

        CONST_LOADS = 10
        LOADS = 4

        def half(c):
            return slice(c * HALF, (c + 1) * HALF)

        def tile_cols(t):
            return slice(t * P, (t + 1) * P)

        def all_pairs(eng, pair):
            pair(0, 0, True, False, True)
            with eng.Fori(0, (PAIRS - 2) // 2) as i:
                pair(i * 2 + 1, 1, True, True, True)
                pair(i * 2 + 2, 0, True, True, True)
            pair(PAIRS - 1, 1, True, True, False)
            pair(PAIRS, 0, False, True, False)

        def all_groups(eng, group):
            groups = TILES // GT
            group(-1, 1, False, False, True)
            group(0, 0, True, False, True)
            group(1, 1, True, True, True)
            with eng.Fori(0, (groups - 4) // 2) as i:
                group(i * 2 + 2, 0, True, True, True)
                group(i * 2 + 3, 1, True, True, True)
            group(groups - 2, 0, True, True, True)
            group(groups - 1, 1, True, True, False)
            group(groups, 0, False, True, False)

        def before(g, j, cur, prev):
            if j >= LAG_DOWN:
                return (g, j - LAG_DOWN) if cur else None
            return (g - 1, j - LAG_DOWN + GT) if prev else None

        def lagging(n, s, lag, cur, prev):
            u = s - lag
            if u >= 0:
                return (n, u, 0) if cur else None
            return (n - 1, u + STEPS, 1) if prev else None

        @block.sync
        def _(sp):
            for b in range(B):
                sp.dma_start(stream[:, b * TB:(b + 1) * TB, :],
                             x_t[:, b * TB:(b + 1) * TB, :]).then_inc(x_loaded[b], 16)
            sp.dma_start(bo_all[:], bo.partition_broadcast(P)).then_inc(w_loaded, 16)
            sp.dma_start(bias_all[:], bias.partition_broadcast(P)).then_inc(w_loaded, 16)
            sp.dma_start(wo[:], Wo_t).then_inc(w_loaded, 16)
            sp.dma_start(wgate[:], gate_wT).then_inc(w_loaded, 16)
            sp.dma_start(wg[:].rearrange("h (e i) -> h e i", e=E),
                         Wg.rearrange("e h i -> h e i")).then_inc(w_loaded, 16)
            sp.dma_start(wu[:].rearrange("h (e i) -> h e i", e=E),
                         Wu.rearrange("e h i -> h e i")).then_inc(w_loaded, 16)
            sp.dma_start(wshared[:, 0:I], Wg_s).then_inc(w_loaded, 16)
            sp.dma_start(wshared[:, I:2 * I], Wu_s).then_inc(w_loaded, 16)
            sp.dma_start(wd[:, 0:KD, :], Wd_t).then_inc(w_loaded, 16)
            sp.dma_start(wd[0:I, KD, :], Wd_s).then_inc(w_loaded, 16)

            def load(parity, c, token):
                sp.dma_start(wcur[parity][:, 0, :], Wq[:, bass.ds(c, P)]).then_inc(pair_loaded[parity], 16)
                sp.dma_start(wcur[parity][:, 1, :], Wkv[:, bass.ds(c, P)]).then_inc(pair_loaded[parity], 16)
                sp.dma_start(wcur[parity][:, 2, :],
                             Wkv[:, INNER:2 * INNER][:, bass.ds(c, P)]).then_inc(pair_loaded[parity], 16)
                sp.dma_start(xcur[parity][:], xT[:, bass.ds(token, N)]).then_inc(pair_loaded[parity], 16)

            def place(m):
                if isinstance(m, int):
                    return m % HP * P, m // HP * N
                return (m & (HP - 1)) * P, ((m >> 3) & (B - 1)) * N

            def stack_q(m, parity):
                for rows, part in ((0, q_high), (DH, q_low)):
                    for h in range(2):
                        sp.dma_start(q_stack[parity][rows:rows + DH, h, :].bitcast(F32),
                                     part[h * DH:(h + 1) * DH, :].bitcast(F32)).then_inc(stacked, 16)

            def stack_k(m, parity):
                for stack, part in ((kh_stack, k_high), (kl_stack, k_low)):
                    for rows in (0, DH):
                        for h in range(2):
                            sp.dma_start(stack[parity][rows:rows + DH, h, :].bitcast(F32),
                                         part[h * DH:(h + 1) * DH, :].bitcast(F32)).then_inc(stacked, 16)

            def prepare(m, parity):
                at_least(sp, low_ready, m * SPLITS + 2)
                stack_q(m, parity)
                at_least(sp, low_ready, m * SPLITS + SPLITS)
                stack_k(m, parity)

            sp.wait_ge(xT_ready, 2 * B)
            for m in range(2):
                load(m, *place(m))
            prepare(0, 0)

            def pair(n, parity, cur, prev, nxt):
                prepare(n + 1, 1 - parity)
                if not isinstance(n, int) or n + 2 < PAIRS:
                    load(parity, *place(n + 2))

            pair(0, 0, True, False, True)
            with sp.Fori(0, (PAIRS - 4) // 2) as i:
                pair(i * 2 + 1, 1, True, True, True)
                pair(i * 2 + 2, 0, True, True, True)
            pair(PAIRS - 3, 1, True, True, True)
            pair(PAIRS - 2, 0, True, True, True)

        @block.gpsimd
        def _(pool):
            nc.gpsimd.memset(ident[:], 0.0)
            nc.gpsimd.memset(causal[:], 1.0)
            nc.gpsimd.memset(earlier[:], 1.0).then_inc(consts_set, 1)
            pool.wait_ge(consts_set, 1)
            nc.gpsimd.affine_select(out=ident[:], in_=ident[:], compare_op=ALU.not_equal, fill=1.0,
                                    base=0, pattern=[[-1, P]], channel_multiplier=1)
            nc.gpsimd.affine_select(out=causal[:], in_=causal[:], compare_op=ALU.is_ge, fill=0.0,
                                    base=0, pattern=[[-1, P]], channel_multiplier=1)
            nc.gpsimd.affine_select(out=earlier[:], in_=earlier[:], compare_op=ALU.is_gt, fill=0.0,
                                    base=0, pattern=[[1, E], [-1, E]],
                                    channel_multiplier=0).then_inc(consts_done, 1)
            pool.wait_ge(w_loaded, CONST_LOADS * 16)
            for b in range(B):
                pool.wait_ge(normed_ready, 2 * b + 2)
                nc.gpsimd.tensor_tensor(
                    stream[:, b * TB:(b + 1) * TB, :], stream[:, b * TB:(b + 1) * TB, :],
                    bo_all[:].unsqueeze(1).to_broadcast([P, TB, D]), ALU.add).then_inc(bo_added, 1)

            def pair(n, parity, cur, prev, nxt):
                if not cur:
                    return
                for s in range(STEPS):
                    t, pr = s // 2, probs[s % P_SLOTS]
                    pool.wait_ge(rden_ready, n * STEPS + s + 1)
                    ins = nc.gpsimd.tensor_tensor(pr[:, 0:P], pr[:, 0:P],
                                                  rden[:, s:s + 1].to_broadcast([P, P]), ALU.mult)
                    if t > 0:
                        ins = nc.gpsimd.tensor_scalar(pr[:, P:(t + 1) * P], pr[:, P:(t + 1) * P],
                                                      rden[:, s:s + 1], 1.0, ALU.mult, ALU.mult)
                    ins.then_inc(scaled, 1)

            all_pairs(pool, pair)

            def weigh(g, par, j):
                n = g * GT + j
                pool.wait_ge(f_sig, n + 1)
                if j == 0:
                    pool.wait_ge(f_weight, g + 1)
                sg = sig[j % 2][:, 0:EI].rearrange("p (e i) -> p e i", e=E)
                nc.gpsimd.tensor_tensor(sg, sg, weight[par][:, j, :].unsqueeze(2).to_broadcast([P, E, I]),
                                        ALU.mult).then_inc(f_sigw, 1)

            with pool.Fori(0, B) as i:
                for par in range(2):
                    for j in range(GT):
                        weigh(i * 2 + par, par, j)

        @block.scalar
        def _(sc):
            sc.wait_ge(var_ready, 1)
            nc.scalar.activation(std[:], var[:], ACT.Sqrt).then_inc(std_ready, 1)
            with sc.Fori(0, B) as b:
                for c in range(2):
                    sc.wait_ge(normed_T, b * 2 + c + 1)
                    nc.scalar.copy(xT[:, bass.ds(b * N + c * HALF, HALF)], t_ps[c][:]).then_inc(xT_ready, 1)

            def take(m, parity, what, c):
                i = FILL[what, c]
                sc.wait_ge(filled, m * FILLS + i + 1)
                if what == "v":
                    if c == 0:
                        at_least(sc, pv_done, (m - 1) * TB)
                    nc.scalar.copy(v[parity][:, c * 4:(c + 1) * 4, :],
                                   m_ps[:].rearrange("p (t d) -> p t d", t=4)).then_inc(act_took, 1)
                    return
                if i == 0:
                    at_least(sc, stacked, m * STACK_DMAS * 16)
                high = q_high if what == "q" else k_high
                nc.scalar.activation(high[:, half(c)], m_ps[:], ACT.Copy,
                                     scale=QSCALE if what == "q" else 1.0).then_inc(act_took, 1)

            for what, c in FILL:
                take(0, 0, what, c)

            def exps(n, s):
                t, slot = s // 2, s % P_SLOTS
                if s >= P_SLOTS:
                    at_least(sc, t_ready, n * GROUPS + groups_before(s - P_SLOTS + 1))
                else:
                    at_least(sc, t_ready, (n - 1) * GROUPS + groups_before(s - P_SLOTS + 1 + STEPS))
                sc.wait_ge(max_ready, n * STEPS + s + 1)
                src, dst = s_ps[s % 2], probs[slot]
                if t > 0:
                    nc.scalar.activation(dst[:, 0:t * P], src[:, 0:t * P], ACT.Exp,
                                         bias=neg_max[:, s:s + 1], accum_out=den_left[:, s:s + 1])
                nc.scalar.activation(dst[:, tile_cols(t)], src[:, tile_cols(t)], ACT.Exp,
                                     bias=neg_max[:, s:s + 1]).then_inc(exp_done, 1)

            def take_T(n, u):
                t = u // 2
                at_least(sc, pv_done, n * TB + t - 1)
                for j0 in range(0, t + 1, 4):
                    k = min(4, t + 1 - j0)
                    g = groups_before(u) + j0 // 4
                    sc.wait_ge(t_ready, n * GROUPS + g + 1)
                    nc.scalar.copy(probsT[u % PT_SLOTS][:, j0 * P:(j0 + k) * P],
                                   t_ps[g % 2][:, 0:k * P]).then_inc(t_taken, 1)

            def pair(n, parity, cur, prev, nxt):
                for s in range(STEPS):
                    if cur:
                        exps(n, s)
                    late = lagging(n, s, LAG_COPY, cur, prev)
                    if late:
                        take_T(late[0], late[1])
                    if s in SHARED and nxt and SHARED[s][0] != "project":
                        take(n + 1, 1 - parity, *SHARED[s])

            all_pairs(sc, pair)

            sc.wait_ge(var_ready, 2)
            nc.scalar.activation(std[:], var[:], ACT.Sqrt).then_inc(std_ready, 1)

            def route_copy(g, par):
                sc.wait_ge(f_T, g + 1)
                at_least(sc, f_up, (g - 1) * GT)
                nc.scalar.copy(ffn_T[par], t_ps[0][:]).then_inc(f_T_taken, 1)

            def route_score(g, par):
                sc.wait_ge(f_logits, g + 1)
                at_least(sc, f_weight, g - 1)
                nc.scalar.activation(scores[par][:].rearrange("p t e -> p (t e)"),
                                     t_ps[1][:, 0:GT * E], ACT.Sigmoid).then_inc(f_scores, 1)

            def expert(g, j):
                n, k = g * GT + j, j % 2
                sc.wait_ge(f_up, n + 1)
                at_least(sc, f_silu, n - 1)
                nc.scalar.activation(sig[k][:, 0:EI], s_ps[k][:, 0:EI], ACT.Sigmoid)
                nc.scalar.activation(sig[k][:, EI:EI + I], sh_ps[k][:, 0:I],
                                     ACT.Sigmoid).then_inc(f_sig, 1)

            def expert_T(g, j):
                n, k = g * GT + j, j % 2
                at_least(sc, f_down, n - 1)
                sc.wait_ge(f_actT, n + 1)
                nc.scalar.copy(actT[k][:, 0:EI], t_ps[0][:])
                nc.scalar.copy(actT[k][0:I, EI:EI + P], sh_ps[k][0:I, 2 * I:2 * I + P])\
                    .then_inc(f_actT_taken, 1)

            def group(g, par, cur, prev, nxt):
                if not cur and nxt:
                    route_copy(g + 1, 1 - par)
                    route_score(g + 1, 1 - par)
                for j in range(GT):
                    late = before(g, j, cur, prev)
                    if late:
                        expert_T(*late)
                    if cur:
                        expert(g, j)
                    if cur and nxt and j == 1:
                        route_copy(g + 1, 1 - par)
                    if cur and nxt and j == 2:
                        route_score(g + 1, 1 - par)
                    if prev and j == 2:
                        store(g - 1, 1 - par)

            def store(g, par):
                sc.wait_ge(f_result, g * GT + GT)
                sc.dma_start(out_t[:, bass.ds(g * GT, GT), :],
                             result[par].rearrange("p (t d) -> p t d", d=D)).then_inc(stored[par], 16)

            all_groups(sc, group)
            for done in stored:
                sc.wait_ge(done, TILES // GT // 2 * 16)

        @block.vector
        def _(dve):
            links = [0]

            def link(ins):
                links[0] += 1
                ins.then_inc(stat_link, 1)
                dve.wait_ge(stat_link, links[0])

            def spread():
                me, mo = stats[:, :, 1], stats[:, :, 4]
                nc.vector.tensor_tensor(mean2[:], me, mo, ALU.add)
                nc.vector.tensor_tensor(diff[:], me, mo, ALU.subtract)
                link(nc.vector.tensor_tensor(m2[:], stats[:, :, 2], stats[:, :, 5], ALU.add))
                nc.vector.tensor_scalar(mean[:], mean2[:], 0.5, None, ALU.mult)
                link(nc.vector.scalar_tensor_tensor(var[:], diff[:], 0.25, diff[:], ALU.mult, ALU.mult))
                link(nc.vector.scalar_tensor_tensor(var[:], m2[:], 1.0 / D, var[:], ALU.mult, ALU.add))
                nc.vector.tensor_scalar(var[:], var[:], LN_EPS, None, ALU.add).then_inc(var_ready, 1)

            def norm(dst, tile):
                return nc.vector.tensor_scalar(dst, stream[:, bass.ds(tile, 1), :],
                                               mean[:, bass.ds(tile, 1)], rstd[:, bass.ds(tile, 1)],
                                               ALU.subtract, ALU.mult)

            def statistics(tiles):
                for t in tiles:
                    last = nc.vector.bn_stats(stats[:, t, :], stream[:, t, :])
                return last

            for b in range(B):
                dve.wait_ge(x_loaded[b], 16)
                last = statistics(range(b * TB, (b + 1) * TB))
            link(last)
            spread()
            dve.wait_ge(std_ready, 1)
            link(nc.vector.reciprocal(rstd[:], std[:]))
            for b in range(B):
                for c in range(2):
                    if b > 0:
                        dve.wait_ge(normed_T, 2 * b - 1 + c)
                    for t in range(4 * c, 4 * c + 4):
                        tile = b * TB + t
                        last = nc.vector.tensor_scalar(normed[:, t, :], stream[:, tile, :],
                                                       mean[:, tile:tile + 1], rstd[:, tile:tile + 1],
                                                       ALU.subtract, ALU.mult)
                    last.then_inc(normed_ready, 1)

            def low(m, what, c):
                dve.wait_ge(act_took, m * FILLS + FILL[what, c] + 1)
                high, rest = (q_high, q_low) if what == "q" else (k_high, k_low)
                nc.vector.scalar_tensor_tensor(
                    rest[:, half(c)], m_ps[:], QSCALE if what == "q" else 1.0,
                    high[:, half(c)].bitcast(F32), ALU.mult, ALU.subtract).then_inc(low_ready, 1)

            for what, c in FILL:
                if what != "v":
                    low(0, what, c)
            dve.wait_ge(consts_done, 1)
            dve.wait_ge(bo_added, B)

            def row_max(n, s):
                dve.wait_ge(s_ready, n * STEPS + s + 1)
                nc.vector.tensor_reduce(neg_max[:, s:s + 1], s_ps[s % 2][:], AX.X, ALU.max,
                                        negate=True).then_inc(max_ready, 1)

            def diagonal(n, s):
                dve.wait_ge(exp_done, n * STEPS + s + 1)
                blk = probs[s % P_SLOTS][:, tile_cols(s // 2)]
                nc.vector.scalar_tensor_tensor(blk, blk, 1.0, causal[:], ALU.mult, ALU.mult,
                                               accum_out=den_diag[:, s:s + 1]).then_inc(diag_done, 1)

            def denominator(n, s):
                dve.wait_ge(diag_done, n * STEPS + s + 1)
                if s // 2 > 0:
                    ins = nc.vector.tensor_scalar(den[:, s:s + 1], den_left[:, s:s + 1],
                                                  den_diag[:, s:s + 1], DEN_EPS, ALU.add, ALU.add)
                else:
                    ins = nc.vector.tensor_scalar(den[:, s:s + 1], den_diag[:, s:s + 1], DEN_EPS,
                                                  None, ALU.add)
                ins.then_inc(den_summed, 1)

            def invert(n, s):
                dve.wait_ge(den_summed, n * STEPS + s + 1)
                nc.vector.reciprocal(rden[:, s:s + 1], den[:, s:s + 1]).then_inc(rden_ready, 1)

            def take_heads(n, par, c):
                dve.wait_ge(pv_done, n * TB + 4 * (c + 1))
                nc.vector.tensor_copy(heads[par][:, half(c)], o_ps[:]).then_inc(o_taken, 1)

            def add(n, c):
                dve.wait_ge(projected, n * 2 + c + 1)
                b = n // HP if isinstance(n, int) else (n >> 3) & (B - 1)
                dst = stream[:, bass.ds(b * TB + 4 * c, 4), :]
                nc.vector.tensor_tensor(dst, m_ps[:].rearrange("p (t d) -> p t d", t=4), dst,
                                        ALU.add).then_inc(added, 1)

            def pair(n, parity, cur, prev, nxt):
                for s in range(STEPS):
                    if cur:
                        row_max(n, s)
                    late = lagging(n, s, 2, cur, prev)
                    if late:
                        denominator(late[0], late[1])
                    late1 = lagging(n, s, 1, cur, prev)
                    if late1:
                        diagonal(late1[0], late1[1])
                    if late:
                        invert(late[0], late[1])
                    if prev and s in (2, 11):
                        add(n - 1, 0 if s == 2 else 1)
                    if nxt and s in (3, 5, 7, 9):
                        low(n + 1, *SHARED[s - 1])
                    if cur and not nxt and s < 3 * TB // 2:
                        statistics(range(2 * s, 2 * s + 2))
                    if cur and s == 15:
                        take_heads(n, parity, 0)
                    if prev and s == 7:
                        take_heads(n - 1, 1 - parity, 1)

            all_pairs(dve, pair)

            dve.wait_ge(added, 2 * PAIRS)
            link(statistics(range(TILES - TB, TILES)))
            spread()
            dve.wait_ge(std_ready, 2)
            link(nc.vector.reciprocal(rstd[:], std[:]))

            def norm_group(g, par):
                at_least(dve, f_T, g - 1)
                for j in range(GT):
                    tile = g * GT + j
                    if isinstance(tile, int):
                        src = stream[:, tile, :]
                        mu, rs = mean[:, tile:tile + 1], rstd[:, tile:tile + 1]
                    else:
                        src = stream[:, bass.ds(tile, 1), :].rearrange("p a d -> p (a d)")
                        mu, rs = mean[:, bass.ds(tile, 1)], rstd[:, bass.ds(tile, 1)]
                    last = nc.vector.tensor_scalar(ffn_in[par][:, j, :], src, mu, rs,
                                                   ALU.subtract, ALU.mult)
                last.then_inc(f_normed, 1)

            def route(g, par):
                ROUTE_LINKS = 15
                count = [0]

                def then(ins):
                    count[0] += 1
                    ins.then_inc(g_link, 1)
                    dve.wait_ge(g_link, g * ROUTE_LINKS + count[0])

                dve.wait_ge(f_scores, g + 1)
                sc_ = scores[par][:]
                then(nc.vector.tensor_tensor(biased[:], sc_,
                                             bias_all[:].unsqueeze(1).to_broadcast([P, GT, E]), ALU.add))
                pairs_ = biased[:].rearrange("p t (g s) -> p t g s", s=GS)
                then(nc.vector.tensor_tensor(group_score[:], pairs_[:, :, :, 0], pairs_[:, :, :, 1],
                                             ALU.add))

                def rank(values, n, tie, above, rank_, before):
                    other = values.unsqueeze(2).to_broadcast([P, GT, n, n])
                    own = values.unsqueeze(3).to_broadcast([P, GT, n, n])
                    nc.vector.tensor_tensor(above[:], other, own, ALU.is_gt)
                    then(nc.vector.tensor_tensor(tie[:], other, own, ALU.is_equal))
                    then(nc.vector.tensor_tensor(tie[:], tie[:],
                                                 before.unsqueeze(1).to_broadcast([P, GT, n, n]),
                                                 ALU.mult))
                    then(nc.vector.tensor_tensor(above[:], above[:], tie[:], ALU.add))
                    then(nc.vector.tensor_reduce(rank_[:], above[:], AX.X, ALU.add))

                rank(group_score[:], NG, tie_g, above_g, rank_g, earlier[:, 0:NG, 0:NG])
                then(nc.vector.tensor_scalar(keep_g[:], rank_g[:], float(TOP_GROUPS), None, ALU.is_lt))
                then(nc.vector.tensor_tensor(choice[:].rearrange("p t (g s) -> p t g s", s=GS), pairs_,
                                             keep_g[:].unsqueeze(3).to_broadcast([P, GT, NG, GS]),
                                             ALU.mult))
                rank(choice[:], E, tie_e, above_e, rank_e, earlier[:])
                then(nc.vector.scalar_tensor_tensor(picked[:], rank_e[:], float(TOPK), sc_, ALU.is_lt,
                                                    ALU.mult))
                then(nc.vector.tensor_reduce(total[:], picked[:], AX.X, ALU.add))
                nc.vector.tensor_scalar(total[:], total[:], TOPK_EPS, None, ALU.add).then_inc(g_link, 1)
                count[0] += 1
                dve.wait_ge(g_link, g * ROUTE_LINKS + count[0])
                assert count[0] == ROUTE_LINKS, count[0]
                nc.vector.reciprocal(rtotal[:], total[:]).then_inc(f_rtotal, 1)
                dve.wait_ge(f_rtotal, g + 1)
                at_least(dve, f_sigw, (g - 1) * GT)
                nc.vector.scalar_tensor_tensor(weight[par][:], picked[:], ROUTED_SCALE,
                                               rtotal[:].unsqueeze(2).to_broadcast([P, GT, E]),
                                               ALU.mult, ALU.mult).then_inc(f_weight, 1)

            def activate(g, j):
                n, k = g * GT + j, j % 2
                dve.wait_ge(f_sig, n + 1)
                dve.wait_ge(f_sigw, n + 1)
                at_least(dve, f_actT, n - 1)
                nc.vector.tensor_tensor(act[k][:, 0:EI], s_ps[k][:, 0:EI], sig[k][:, 0:EI], ALU.mult)
                nc.vector.tensor_tensor(act[k][:, EI:EI + I], sh_ps[k][:, 0:I],
                                        sig[k][:, EI:EI + I], ALU.mult).then_inc(f_silu, 1)
                dve.wait_ge(f_silu, n + 1)
                nc.vector.tensor_tensor(act[k][:, 0:EI], s_ps[k][:, EI:2 * EI], act[k][:, 0:EI], ALU.mult)
                nc.vector.tensor_tensor(act[k][:, EI:EI + I], sh_ps[k][:, I:2 * I],
                                        act[k][:, EI:EI + I], ALU.mult).then_inc(f_act, 1)

            def finish(g, par, j):
                n = g * GT + j
                dve.wait_ge(f_down, n + 1)
                if j == 0:
                    at_least(dve, stored[par], (g >> 1) * 16)
                if isinstance(n, int):
                    src = stream[:, n, :]
                else:
                    src = stream[:, bass.ds(n, 1), :].rearrange("p a d -> p (a d)")
                nc.vector.tensor_tensor(result[par][:, tile_cols(j)], t_ps[1][:, P:2 * P], src, ALU.add)\
                    .then_inc(f_result, 1)

            def group(g, par, cur, prev, nxt):
                if not cur and nxt:
                    norm_group(g + 1, 1 - par)
                    route(g + 1, 1 - par)
                for j in range(GT):
                    late = before(g, j, cur, prev)
                    if late:
                        finish(late[0], par if late[0] is g else 1 - par, late[1])
                    if cur:
                        activate(g, j)
                    if cur and nxt and j == 0:
                        norm_group(g + 1, 1 - par)
                    if cur and nxt and j == 2:
                        route(g + 1, 1 - par)

            all_groups(dve, group)

        @block.tensor
        def _(pe):
            pe.wait_ge(consts_done, 1)
            for b in range(B):
                for c in range(2):
                    pe.wait_ge(normed_ready, 2 * b + c + 1)
                    if b > 0:
                        pe.wait_ge(xT_ready, 2 * b - 1 + c)
                    for j in range(4):
                        last = nc.tensor.transpose(t_ps[c][:, tile_cols(j)], normed[:, 4 * c + j, :],
                                                   ident[:])
                    last.then_inc(normed_T, 1)

            def fill(m, parity, what, c):
                if what == "v":
                    for j in range(4):
                        last = nc.tensor.matmul(m_ps[:, tile_cols(j)], xcur[parity][:, tile_cols(4 * c + j)],
                                                wcur[parity][:, 2, :], start=True, stop=True)
                else:
                    last = nc.tensor.matmul(m_ps[:], wcur[parity][:, 0 if what == "q" else 1, :],
                                            xcur[parity][:, half(c)], start=True, stop=True)
                last.then_inc(filled, 1)

            pe.wait_ge(pair_loaded[0], LOADS * 16)
            for what, c in FILL:
                i = FILL[what, c]
                if 0 < i <= SPLITS:
                    pe.wait_ge(low_ready, i)
                elif i > SPLITS:
                    pe.wait_ge(act_took, i)
                fill(0, 0, what, c)

            def scores_of(n, parity, s):
                t, h = s // 2, s % 2
                if s == 0:
                    pe.wait_ge(stacked, (n * STACK_DMAS + STACK_DMAS) * 16)
                at_least(pe, exp_done, n * STEPS + s - 1)
                qs = q_stack[parity][:, h, tile_cols(t)]
                for c in range(2):
                    nc.tensor.matmul(s_ps[s % 2][:, half(c)], qs, kh_stack[parity][:, h, half(c)],
                                     start=True, stop=False)
                    last = nc.tensor.matmul(s_ps[s % 2][:, half(c)], qs, kl_stack[parity][:, h, half(c)],
                                            start=False, stop=True)
                last.then_inc(s_ready, 1)

            def transposes(n, u):
                pe.wait_ge(scaled, n * STEPS + u + 1)
                t = u // 2
                for j0 in range(0, t + 1, 4):
                    g = groups_before(u) + j0 // 4
                    at_least(pe, t_taken, n * GROUPS + g - 1)
                    for j in range(j0, min(j0 + 4, t + 1)):
                        last = nc.tensor.transpose(t_ps[g % 2][:, tile_cols(j - j0)],
                                                   probs[u % P_SLOTS][:, tile_cols(j)], ident[:])
                    last.then_inc(t_ready, 1)

            def values(n, parity, t):
                pe.wait_ge(t_taken, n * GROUPS + groups_before(2 * t + 2))
                if t == 0:
                    pe.wait_ge(act_took, n * FILLS + FILLS)
                if t % 4 == 0:
                    at_least(pe, o_taken, n * 2 + t // 4)
                for j in range(t + 1):
                    for h in range(2):
                        last = nc.tensor.matmul(
                            o_ps[h * DH:(h + 1) * DH, tile_cols(t % 4)], v[parity][:, j, h * DH:(h + 1) * DH],
                            probsT[(2 * t + h) % PT_SLOTS][:, tile_cols(j)], start=(j == 0), stop=(j == t))
                last.then_inc(pv_done, 1)

            def project(n, parity, c):
                pe.wait_ge(o_taken, n * 2 + c + 1)
                if isinstance(n, int):
                    w = wo[:, n % HP, :]
                else:
                    w = wo[:].rearrange("p k d -> p (k d)")[:, bass.ds((n & (HP - 1)) * D, D)]
                for j in range(4):
                    last = nc.tensor.matmul(m_ps[:, tile_cols(j)], heads[parity][:, tile_cols(4 * c + j)],
                                            w, start=True, stop=True)
                last.then_inc(projected, 1)

            def shared(n, parity, s, cur, prev, nxt):
                what, c = SHARED[s]
                if what == "project":
                    if not prev:
                        return
                    if c == 0 and cur:
                        pe.wait_ge(act_took, n * FILLS + FILLS)
                    elif c == 0:
                        pe.wait_ge(added, 2 * (n - 1))
                    elif nxt:
                        pe.wait_ge(low_ready, (n + 1) * SPLITS + SPLITS)
                    else:
                        pe.wait_ge(added, 2 * (n - 1) + 1)
                    project(n - 1, 1 - parity, c)
                    return
                if not nxt:
                    return
                i = FILL[what, c]
                if i == 0:
                    before = (n + 1) // 2 if isinstance(n, int) else (n + 1) >> 1
                    pe.wait_ge(pair_loaded[1 - parity], before * LOADS * 16 + LOADS * 16)
                    if prev:
                        pe.wait_ge(added, 2 * (n - 1) + 1)
                    else:
                        pe.wait_ge(act_took, (n + 1) * FILLS)
                elif i < SPLITS:
                    pe.wait_ge(low_ready, (n + 1) * SPLITS + i)
                elif i == SPLITS:
                    pe.wait_ge(low_ready, (n + 1) * SPLITS + SPLITS)
                    at_least(pe, added, 2 * n)
                else:
                    pe.wait_ge(act_took, (n + 1) * FILLS + i)
                fill(n + 1, 1 - parity, what, c)

            def pair(n, parity, cur, prev, nxt):
                for s in range(STEPS):
                    if cur:
                        scores_of(n, parity, s)
                    late = lagging(n, s, LAG_T, cur, prev)
                    if late:
                        transposes(late[0], late[1])
                    late = lagging(n, s, LAG_PV, cur, prev)
                    if late and late[1] % 2 == 1:
                        values(late[0], parity ^ late[2], late[1] // 2)
                    if s in SHARED:
                        shared(n, parity, s, cur, prev, nxt)

            all_pairs(pe, pair)

            def route_T(g, par):
                pe.wait_ge(f_normed, g + 1)
                at_least(pe, f_actT_taken, (g - 1) * GT)
                for j in range(GT):
                    last = nc.tensor.transpose(t_ps[0][:, tile_cols(j)], ffn_in[par][:, j, :], ident[:])
                last.then_inc(f_T, 1)

            def route_logits(g, par):
                pe.wait_ge(f_T_taken, g + 1)
                at_least(pe, f_result, (g - 1) * GT + 1)
                for j in range(GT):
                    last = nc.tensor.matmul(t_ps[1][:, j * E:(j + 1) * E], ffn_T[par][:, tile_cols(j)],
                                            wgate[:], start=True, stop=True)
                last.then_inc(f_logits, 1)

            def up(g, par, j):
                n, k = g * GT + j, j % 2
                if j == 0:
                    pe.wait_ge(f_T_taken, g + 1)
                at_least(pe, f_act, n - 1)
                hT = ffn_T[par][:, tile_cols(j)]
                nc.tensor.matmul(s_ps[k][:, 0:EI], hT, wg[:], start=True, stop=True)
                nc.tensor.matmul(s_ps[k][:, EI:2 * EI], hT, wu[:], start=True, stop=True)
                at_least(pe, f_actT_taken, n - 1)
                nc.tensor.matmul(sh_ps[k][:, 0:2 * I], hT, wshared[:], start=True,
                                 stop=True).then_inc(f_up, 1)

            def act_T(g, j, routed):
                n, k = g * GT + j, j % 2
                pe.wait_ge(f_act, n + 1)
                at_least(pe, f_actT_taken, n)
                at_least(pe, f_T_taken, routed)
                for b in range(KD):
                    nc.tensor.transpose(t_ps[0][:, tile_cols(b)], act[k][:, tile_cols(b)], ident[:])
                nc.tensor.transpose(sh_ps[k][0:I, 2 * I:2 * I + P], act[k][:, EI:EI + I], ident[:])\
                    .then_inc(f_actT, 1)

            def down(g, j, scored):
                n, k = g * GT + j, j % 2
                pe.wait_ge(f_actT_taken, n + 1)
                at_least(pe, f_result, n)
                at_least(pe, f_scores, scored)
                for b in range(KD):
                    nc.tensor.matmul(t_ps[1][:, P:2 * P], actT[k][:, tile_cols(b)], wd[:, b, :],
                                     start=(b == 0), stop=False)
                nc.tensor.matmul(t_ps[1][:, P:2 * P], actT[k][0:I, EI:EI + P], wd[0:I, KD, :],
                                 start=False, stop=True).then_inc(f_down, 1)

            def group(g, par, cur, prev, nxt):
                if not cur and nxt:
                    route_T(g + 1, 1 - par)
                    route_logits(g + 1, 1 - par)
                for j in range(GT):
                    late = before(g, j, cur, prev)
                    if late:
                        act_T(*late, g + 2 if (nxt and j >= 2) else g + 1 if cur else g)
                    if cur:
                        up(g, par, j)
                    if late:
                        down(*late, g + 2 if (nxt and j >= 3) else g + 1 if cur else g)
                    if cur and nxt and j == 1:
                        route_T(g + 1, 1 - par)
                    if cur and nxt and j == 2:
                        route_logits(g + 1, 1 - par)

            all_groups(pe, group)


_INS = ["L0_attn_x", "L0_attn_Wq", "L0_attn_Wkv", "L0_attn_Wo", "L0_attn_bo", "L0_ffn_gate_w",
        "L0_ffn_correction_bias", "L0_ffn_Wg", "L0_ffn_Wu", "L0_ffn_Wd", "L0_ffn_Wg_s",
        "L0_ffn_Wu_s", "L0_ffn_Wd_s"]


def kernel(**inputs):
    import concourse.bacc as bacc
    import numpy as np
    from concourse.bass_utils import run_bass_kernel_spmd

    nc = bacc.Bacc("TRN2", target_bir_lowering=False, num_devices=1)
    arrays, args = {}, []
    for name in _INS:
        a = np.asarray(inputs[name])
        if name == "L0_ffn_gate_w":
            a = a.T
        a = np.ascontiguousarray(a)
        arrays[f"in_{name}"] = a
        args.append(nc.dram_tensor(f"in_{name}", a.shape, mybir.dt.from_np(a.dtype),
                                   kind="ExternalInput").ap())
    out = nc.dram_tensor("out", inputs["L0_attn_x"].shape, F32, kind="ExternalOutput").ap()
    build(nc, *args, out)
    r = run_bass_kernel_spmd(nc, [arrays], core_ids=[0])
    return r.results[0]["out"]
```

```python
from contextlib import ExitStack

import concourse.bass as bass
from concourse import mybir
from concourse.alu_op_type import AluOpType as ALU

F32 = mybir.dt.float32
F32R = mybir.dt.float32r
ACT = mybir.ActivationFunctionType
AX = mybir.AxisListType

P = 128
BANK = 512
LN_EPS = 1e-5
DEN_EPS = 1e-8
TOPK_EPS = 1e-20
ROUTED_SCALE = 2.5
TOPK, TOP_GROUPS = 4, 2

STEPS = 16
P_SLOTS = 8
LAG_T = 5
LAG_COPY = 5
LAG_PV = (6, 7)
LAG_DOWN = 2
SHARED = {0: ("project", 0), 1: ("q", 0), 3: ("q", 1), 5: ("k", 0), 7: ("k", 1),
          9: ("project", 1), 11: ("v", 0), 13: ("v", 1)}
HIGH_STEPS = (8, 9, 11)
LOW_STEPS = (10, 11, 12)
FILL = {("q", 0): 0, ("q", 1): 1, ("k", 0): 2, ("k", 1): 3, ("v", 0): 4, ("v", 1): 5}
FILLS = len(FILL)
SPLITS = 4


def groups_before(step):
    return sum(1 if s // 2 < 4 else 2 for s in range(step))


GROUPS = groups_before(STEPS)


def at_least(eng, sem, value):
    if isinstance(value, int) and value <= 0:
        return
    eng.wait_ge(sem, value)


def build(nc, x, Wq, Wkv, Wo, bo, gate_wT, bias, Wg, Wu, Wd, Wg_s, Wu_s, Wd_s, out):
    B, N, D = x.shape
    INNER = Wq.shape[1]
    DH = 64
    HP = INNER // P
    PAIRS = B * HP
    TB = N // P
    TILES = B * TB
    TT = TB // 2
    E, _, I = Wg.shape
    EI = E * I
    KD = EI // P
    NG = 4
    GS = E // NG
    QSCALE = float(DH) ** -0.5
    HALF = N // 2
    GT = HALF // P
    assert D == P and N == 2 * BANK and STEPS == 2 * TB and EI == BANK and HP == 8

    x_t = x.rearrange("b (t p) d -> p (b t) d", p=P)
    out_t = out.rearrange("b (t p) d -> p (b t) d", p=P)
    STACK_DMAS = 12
    Wo_t = Wo.rearrange("(k p) d -> p k d", p=P)
    Wd_t = Wd.rearrange("e i h -> (e i) h").rearrange("(k p) h -> p k h", p=P)

    ctx = ExitStack()
    with ctx:
        def sb(name, shape, dt=F32):
            return ctx.enter_context(nc.sbuf_tensor(name, shape, dt))

        def pb(name, shape):
            return ctx.enter_context(nc.psum_tensor(name, shape, F32))

        def sem(name):
            return ctx.enter_context(nc.semaphore(name))

        ident = sb("ident", [P, P])
        causal = sb("causal", [P, P])
        earlier = sb("earlier", [P, E, E])
        bo_all = sb("bo_all", [P, D])
        bias_all = sb("bias_all", [P, E])
        wo = sb("wo", [P, HP, D])
        wgate = sb("wgate", [P, E])
        wshared = sb("wshared", [P, 2 * I])
        wd = sb("wd", [P, KD + 1, D])

        stream = sb("stream", [P, TILES, D])
        xT = sb("xT", [P, B * N])
        stats = sb("stats", [P, TILES, 6])
        mean2 = sb("mean2", [P, TILES])
        mean = sb("mean", [P, TILES])
        diff = sb("diff", [P, TILES])
        var = sb("var", [P, TILES])
        m2 = sb("m2", [P, TILES])
        std = sb("std", [P, TILES])
        rstd = sb("rstd", [P, TILES])

        xcur = [sb(f"xcur{i}", [P, N]) for i in range(2)]
        wcur = [sb(f"wcur{i}", [P, 3, P]) for i in range(2)]
        x_high, x_low = sb("x_high", [P, N], F32R), sb("x_low", [P, N], F32R)
        wqk_high, wqk_low = sb("wqk_high", [P, 2, P], F32R), sb("wqk_low", [P, 2, P], F32R)
        q_high, q_low = sb("q_high", [P, N], F32R), sb("q_low", [P, N], F32R)
        k_high, k_low = sb("k_high", [P, N], F32R), sb("k_low", [P, N], F32R)
        q_stack = [sb(f"q_stack{i}", [P, 2, N], F32R) for i in range(2)]
        kh_stack = [sb(f"kh_stack{i}", [P, 2, N], F32R) for i in range(2)]
        kl_stack = [sb(f"kl_stack{i}", [P, 2, N], F32R) for i in range(2)]
        v = [sb(f"v{i}", [P, TB, P]) for i in range(2)]
        probs = [sb(f"probs{i}", [P, N]) for i in range(P_SLOTS)]
        probsT = [[sb(f"probsT{i}{h}", [P, (TB - 2, TB)[i], 2 * P]) for h in range(2)] for i in range(2)]
        heads = sb("heads", [P, N])
        normed = probs[7][:].rearrange("p (t d) -> p t d", d=D)
        neg_max = sb("neg_max", [P, STEPS])
        den_left = sb("den_left", [P, STEPS])
        den_diag = sb("den_diag", [P, STEPS])
        den = sb("den", [P, STEPS])
        rden = sb("rden", [P, STEPS])

        flat = [[b[:].rearrange("p j q -> p (j q)")[:, 0:GT * P] for b in two] for two in probsT]
        ffn_in = [flat[0][i].rearrange("p (t d) -> p t d", d=D) for i in range(2)]
        ffn_T = flat[1]
        w_high, w_low = q_high, q_low
        w_wide = xcur[0][:]
        ffn_T_high = [k_high[:, i * GT * P:(i + 1) * GT * P] for i in range(2)]
        ffn_T_low = [k_low[:, i * GT * P:(i + 1) * GT * P] for i in range(2)]
        sig = [probs[i][:, 0:EI + I] for i in range(2)]
        act = [probs[2 + i][:, 0:EI + I] for i in range(2)]
        actT = [probs[4 + i][:, 0:(KD + 1) * P] for i in range(2)]
        result = [xcur[i][:, 0:GT * D] for i in range(2)]
        scores = [sb(f"scores{i}", [P, GT, E]) for i in range(2)]
        biased = sb("biased", [P, GT, E])
        group_score = sb("group_score", [P, GT, NG])
        tie_g, above_g = sb("tie_g", [P, GT, NG, NG]), sb("above_g", [P, GT, NG, NG])
        rank_g, keep_g = sb("rank_g", [P, GT, NG]), sb("keep_g", [P, GT, NG])
        choice = sb("choice", [P, GT, E])
        tie_e, above_e = sb("tie_e", [P, GT, E, E]), sb("above_e", [P, GT, E, E])
        rank_e = sb("rank_e", [P, GT, E])
        picked = sb("picked", [P, GT, E])
        total = sb("total", [P, GT])
        rtotal = sb("rtotal", [P, GT])
        weight = [sb(f"weight{i}", [P, GT, E]) for i in range(2)]

        s_ps = [pb(f"s_ps{i}", [P, N]) for i in range(2)]
        t_ps = [pb(f"t_ps{i}", [P, BANK]) for i in range(2)]
        o_ps = pb("o_ps", [P, BANK])
        m_ps = pb("m_ps", [P, BANK])

        sh_ps = [o_ps, m_ps]
        logits_ps = sh_ps[1][:, 2 * I + P:2 * I + P + GT * E]

        first_bank = {("q", 0): s_ps[0][:, 0:BANK], ("q", 1): s_ps[0][:, BANK:2 * BANK],
                      ("k", 0): s_ps[1][:, 0:BANK], ("k", 1): s_ps[1][:, BANK:2 * BANK],
                      ("v", 0): o_ps[:], ("v", 1): m_ps[:]}

        x_loaded = [sem(f"x_loaded{b}") for b in range(B)]
        w_loaded = sem("w_loaded")
        first_w_loaded = sem("first_w_loaded")
        consts_set = sem("consts_set")
        consts_done = sem("consts_done")
        bo_added = sem("bo_added")
        stat_link = sem("stat_link")
        var_ready = sem("var_ready")
        std_ready = sem("std_ready")
        normed_ready = sem("normed_ready")
        normed_T = sem("normed_T")
        xT_ready = sem("xT_ready")

        pair_loaded = [sem(f"pair_loaded{i}") for i in range(2)]
        parts_high = sem("parts_high")
        parts_low = sem("parts_low")
        filled = sem("filled")
        act_took = sem("act_took")
        low_ready = sem("low_ready")
        stacked = sem("stacked")
        s_ready = sem("s_ready")
        max_ready = sem("max_ready")
        exp_done = sem("exp_done")
        diag_done = sem("diag_done")
        den_summed = sem("den_summed")
        rden_ready = sem("rden_ready")
        scaled = sem("scaled")
        t_ready = sem("t_ready")
        t_taken = sem("t_taken")
        pv_done = sem("pv_done")
        o_taken = sem("o_taken")
        projected = sem("projected")
        added = sem("added")

        f_normed = sem("f_normed")
        f_T = sem("f_T")
        f_T_taken = sem("f_T_taken")
        f_T_low = sem("f_T_low")
        w_wide_loaded = sem("w_wide_loaded")
        w_high_ready = sem("w_high_ready")
        w_low_ready = sem("w_low_ready")
        f_logits = sem("f_logits")
        f_scores = sem("f_scores")
        g_link = sem("g_link")
        f_rtotal = sem("f_rtotal")
        f_weight = sem("f_weight")
        f_gates = sem("f_gates")
        f_up = sem("f_up")
        f_sig = sem("f_sig")
        f_sig_shared = sem("f_sig_shared")
        f_sigw = sem("f_sigw")
        f_silu = sem("f_silu")
        f_act = sem("f_act")
        f_actT = sem("f_actT")
        f_actT_taken = sem("f_actT_taken")
        f_down = sem("f_down")
        f_result = sem("f_result")
        stored = [sem(f"stored{i}") for i in range(2)]

        block = ctx.enter_context(nc.Block())

        CONST_LOADS = 8
        LOADS = 4

        def half(c):
            return slice(c * HALF, (c + 1) * HALF)

        def tile_cols(t):
            return slice(t * P, (t + 1) * P)

        def all_pairs(eng, pair):
            pair(0, 0, True, False, True)
            with eng.Fori(0, (PAIRS - 4) // 2) as i:
                pair(i * 2 + 1, 1, True, True, True)
                pair(i * 2 + 2, 0, True, True, True)
            pair(PAIRS - 3, 1, True, True, True)
            pair(PAIRS - 2, 0, True, True, True)
            pair(PAIRS - 1, 1, True, True, False)
            pair(PAIRS, 0, False, True, False)

        def all_groups(eng, group):
            groups = TILES // GT
            group(-1, 1, False, False, True)
            group(0, 0, True, False, True)
            group(1, 1, True, True, True)
            with eng.Fori(0, (groups - 4) // 2) as i:
                group(i * 2 + 2, 0, True, True, True)
                group(i * 2 + 3, 1, True, True, True)
            group(groups - 2, 0, True, True, True)
            group(groups - 1, 1, True, True, False)
            group(groups, 0, False, True, False)

        def before(g, j, cur, prev):
            if j >= LAG_DOWN:
                return (g, j - LAG_DOWN) if cur else None
            return (g - 1, j - LAG_DOWN + GT) if prev else None

        def parts(parity, i):
            if i < 2:
                return xcur[parity][:, half(i)], x_high[:, half(i)], x_low[:, half(i)]
            return wcur[parity][:, 0:2, :], wqk_high[:], wqk_low[:]

        def splits_after(n, cur):
            return cur and (not isinstance(n, int) or n + 2 < PAIRS)

        def lagging(n, s, lag, cur, prev):
            u = s - lag
            if u >= 0:
                return (n, u, 0) if cur else None
            return (n - 1, u + STEPS, 1) if prev else None

        @block.sync
        def _(sp):
            def load_w(parity, c, done):
                sp.dma_start(wcur[parity][:, 0, :], Wq[:, bass.ds(c, P)]).then_inc(done, 16)
                sp.dma_start(wcur[parity][:, 1, :], Wkv[:, bass.ds(c, P)]).then_inc(done, 16)
                sp.dma_start(wcur[parity][:, 2, :],
                             Wkv[:, INNER:2 * INNER][:, bass.ds(c, P)]).then_inc(done, 16)

            for b in range(B):
                sp.dma_start(stream[:, b * TB:(b + 1) * TB, :],
                             x_t[:, b * TB:(b + 1) * TB, :]).then_inc(x_loaded[b], 16)
                if b == 0:
                    load_w(0, 0, first_w_loaded)
            sp.dma_start(bo_all[:], bo.partition_broadcast(P)).then_inc(w_loaded, 16)
            sp.dma_start(bias_all[:], bias.partition_broadcast(P)).then_inc(w_loaded, 16)
            sp.dma_start(wo[:], Wo_t).then_inc(w_loaded, 16)
            sp.dma_start(wgate[:], gate_wT).then_inc(w_loaded, 16)
            sp.dma_start(wshared[:, 0:I], Wg_s).then_inc(w_loaded, 16)
            sp.dma_start(wshared[:, I:2 * I], Wu_s).then_inc(w_loaded, 16)
            sp.dma_start(wd[:, 0:KD, :], Wd_t).then_inc(w_loaded, 16)
            sp.dma_start(wd[0:I, KD, :], Wd_s).then_inc(w_loaded, 16)

            def load(parity, c, token):
                load_w(parity, c, pair_loaded[parity])
                sp.dma_start(xcur[parity][:], xT[:, bass.ds(token, N)]).then_inc(pair_loaded[parity], 16)

            def place(m):
                if isinstance(m, int):
                    return m % HP * P, m // HP * N
                return (m & (HP - 1)) * P, ((m >> 3) & (B - 1)) * N

            def stack_q(m, parity):
                for rows, part in ((0, q_high), (DH, q_low)):
                    for h in range(2):
                        sp.dma_start(q_stack[parity][rows:rows + DH, h, :].bitcast(F32),
                                     part[h * DH:(h + 1) * DH, :].bitcast(F32)).then_inc(stacked, 16)

            def stack_k(m, parity):
                for stack, part in ((kh_stack, k_high), (kl_stack, k_low)):
                    for rows in (0, DH):
                        for h in range(2):
                            sp.dma_start(stack[parity][rows:rows + DH, h, :].bitcast(F32),
                                         part[h * DH:(h + 1) * DH, :].bitcast(F32)).then_inc(stacked, 16)

            def prepare_q(m, parity):
                at_least(sp, low_ready, m * SPLITS + 2)
                stack_q(m, parity)

            def prepare_k(m, parity):
                at_least(sp, low_ready, m * SPLITS + SPLITS)
                stack_k(m, parity)

            sp.wait_ge(xT_ready, 2)
            load(1, *place(1))
            prepare_q(0, 0)
            prepare_k(0, 0)
            sp.wait_ge(xT_ready, 2 * B)

            def pair(n, parity, cur, prev, nxt):
                prepare_q(n + 1, 1 - parity)
                if not isinstance(n, int) or n + 2 < PAIRS:
                    load(parity, *place(n + 2))
                prepare_k(n + 1, 1 - parity)

            pair(0, 0, True, False, True)
            with sp.Fori(0, (PAIRS - 4) // 2) as i:
                pair(i * 2 + 1, 1, True, True, True)
                pair(i * 2 + 2, 0, True, True, True)
            pair(PAIRS - 3, 1, True, True, True)
            pair(PAIRS - 2, 0, True, True, True)

            for c, w in ((0, Wg), (1, Wu)):
                sp.dma_start(w_wide[:, c * EI:(c + 1) * EI].rearrange("h (e i) -> h e i", e=E),
                             w.rearrange("e h i -> h e i")).then_inc(w_wide_loaded, 16)

        @block.gpsimd
        def _(pool):
            nc.gpsimd.memset(ident[:], 0.0)
            nc.gpsimd.memset(causal[:], 1.0)
            nc.gpsimd.memset(earlier[:], 1.0).then_inc(consts_set, 1)
            pool.wait_ge(consts_set, 1)
            nc.gpsimd.affine_select(out=ident[:], in_=ident[:], compare_op=ALU.not_equal, fill=1.0,
                                    base=0, pattern=[[-1, P]], channel_multiplier=1)
            nc.gpsimd.affine_select(out=causal[:], in_=causal[:], compare_op=ALU.is_ge, fill=0.0,
                                    base=0, pattern=[[-1, P]], channel_multiplier=1)
            nc.gpsimd.affine_select(out=earlier[:], in_=earlier[:], compare_op=ALU.is_gt, fill=0.0,
                                    base=0, pattern=[[1, E], [-1, E]],
                                    channel_multiplier=0).then_inc(consts_done, 1)
            pool.wait_ge(w_loaded, CONST_LOADS * 16)
            for b in range(B):
                pool.wait_ge(normed_ready, 2 * b + 2)
                nc.gpsimd.tensor_tensor(
                    stream[:, b * TB:(b + 1) * TB, :], stream[:, b * TB:(b + 1) * TB, :],
                    bo_all[:].unsqueeze(1).to_broadcast([P, TB, D]), ALU.add).then_inc(bo_added, 1)

            def low_part(m, parity, i):
                src, high, rest = parts(parity, i)
                pool.wait_ge(parts_high, (m - 1) * 3 + i + 1)
                nc.gpsimd.tensor_tensor(rest, src, high.bitcast(F32), ALU.subtract)\
                    .then_inc(parts_low, 1)

            for i in range(3):
                low_part(1, 1, i)

            def pair(n, parity, cur, prev, nxt):
                if not cur:
                    return
                for s in range(STEPS):
                    t, pr = s // 2, probs[s % P_SLOTS]
                    pool.wait_ge(rden_ready, n * STEPS + s + 1)
                    ins = nc.gpsimd.tensor_tensor(pr[:, 0:P], pr[:, 0:P],
                                                  rden[:, s:s + 1].to_broadcast([P, P]), ALU.mult)
                    if t > 0:
                        ins = nc.gpsimd.tensor_scalar(pr[:, P:(t + 1) * P], pr[:, P:(t + 1) * P],
                                                      rden[:, s:s + 1], 1.0, ALU.mult, ALU.mult)
                    ins.then_inc(scaled, 1)
                    if s in LOW_STEPS and splits_after(n, cur):
                        low_part(n + 2, parity, LOW_STEPS.index(s))

            all_pairs(pool, pair)

            def weigh(g, par, j):
                n = g * GT + j
                pool.wait_ge(f_sig, n + 1)
                if j == 0:
                    pool.wait_ge(f_weight, g + 1)
                sg = sig[j % 2][:, 0:EI].rearrange("p (e i) -> p e i", e=E)
                nc.gpsimd.tensor_tensor(sg, sg, weight[par][:, j, :].unsqueeze(2).to_broadcast([P, E, I]),
                                        ALU.mult).then_inc(f_sigw, 1)

            def low_T(g, par):
                pool.wait_ge(f_T_taken, g + 1)
                nc.gpsimd.tensor_tensor(ffn_T_low[par], ffn_T[par], ffn_T_high[par].bitcast(F32),
                                        ALU.subtract).then_inc(f_T_low, 1)

            def group(g, par, cur, prev, nxt):
                if not cur and nxt:
                    low_T(g + 1, 1 - par)
                for j in range(GT):
                    if cur:
                        weigh(g, par, j)
                    if cur and nxt and j == 1:
                        low_T(g + 1, 1 - par)

            all_groups(pool, group)

        @block.scalar
        def _(sc):
            def take_xT(b):
                for c in range(2):
                    sc.wait_ge(normed_T, b * 2 + c + 1)
                    nc.scalar.copy(xT[:, bass.ds(b * N + c * HALF, HALF)], t_ps[c][:]).then_inc(xT_ready, 1)

            def take(m, parity, what, c, bank=m_ps[:]):
                i = FILL[what, c]
                sc.wait_ge(filled, m * FILLS + i + 1)
                if what == "v":
                    if c == 0:
                        at_least(sc, pv_done, (m - 1) * TT)
                    nc.scalar.copy(v[parity][:, c * 4:(c + 1) * 4, :],
                                   bank.rearrange("p (t d) -> p t d", t=4)).then_inc(act_took, 1)
                    return
                if (what, c) == ("q", 0):
                    at_least(sc, stacked, m * STACK_DMAS * 16)
                high = q_high if what == "q" else k_high
                nc.scalar.activation(high[:, half(c)], bank, ACT.Copy,
                                     scale=QSCALE if what == "q" else 1.0).then_inc(act_took, 1)

            def high_part(m, parity, i):
                if i == 0:
                    sc.wait_ge(pair_loaded[parity], ((m + 1) >> 1) * LOADS * 16)
                    at_least(sc, filled, (m - 1) * FILLS + FILL["k", 1] + 1)
                src, high, _ = parts(parity, i)
                nc.scalar.copy(high, src).then_inc(parts_high, 1)

            sc.wait_ge(var_ready, 1)
            nc.scalar.activation(std[:, 0:TB], var[:, 0:TB], ACT.Sqrt).then_inc(std_ready, 1)
            take_xT(0)
            sc.wait_ge(var_ready, 2)
            nc.scalar.activation(std[:, TB:TILES], var[:, TB:TILES], ACT.Sqrt).then_inc(std_ready, 1)
            for what, c in FILL:
                take(0, 0, what, c, first_bank[what, c])
            for b in range(1, B):
                take_xT(b)
            for i in range(3):
                high_part(1, 1, i)

            def exps(n, s):
                t, slot = s // 2, s % P_SLOTS
                if s >= P_SLOTS:
                    at_least(sc, t_ready, n * GROUPS + groups_before(s - P_SLOTS + 1))
                else:
                    at_least(sc, t_ready, (n - 1) * GROUPS + groups_before(s - P_SLOTS + 1 + STEPS))
                sc.wait_ge(max_ready, n * STEPS + s + 1)
                src, dst = s_ps[s % 2], probs[slot]
                if t > 0:
                    nc.scalar.activation(dst[:, 0:t * P], src[:, 0:t * P], ACT.Exp,
                                         bias=neg_max[:, s:s + 1], accum_out=den_left[:, s:s + 1])
                nc.scalar.activation(dst[:, tile_cols(t)], src[:, tile_cols(t)], ACT.Exp,
                                     bias=neg_max[:, s:s + 1]).then_inc(exp_done, 1)

            def take_T(n, u):
                t, two = u // 2, u // 4
                buf = probsT[two % 2][u % 2]
                at_least(sc, pv_done, n * TT + two - 1)
                for j0 in range(0, t + 1, 4):
                    k = min(4, t + 1 - j0)
                    g = groups_before(u) + j0 // 4
                    sc.wait_ge(t_ready, n * GROUPS + g + 1)
                    nc.scalar.copy(buf[:, j0:j0 + k, tile_cols(t % 2)],
                                   t_ps[g % 2][:, 0:k * P].rearrange("p (j q) -> p j q", q=P))\
                        .then_inc(t_taken, 1)

            def pair(n, parity, cur, prev, nxt):
                for s in range(STEPS):
                    late = lagging(n, s, LAG_COPY, cur, prev)
                    if late:
                        take_T(late[0], late[1])
                    if cur:
                        exps(n, s)
                    if not cur and s == LAG_COPY:
                        sc.wait_ge(var_ready, 3)
                        nc.scalar.activation(std[:, 0:TILES - TB], var[:, 0:TILES - TB],
                                             ACT.Sqrt).then_inc(std_ready, 1)
                    if s in HIGH_STEPS and splits_after(n, cur):
                        high_part(n + 2, parity, HIGH_STEPS.index(s))
                    if cur and not nxt and s == 8:
                        sc.wait_ge(w_wide_loaded, 2 * 16)
                        sc.wait_ge(stacked, PAIRS * STACK_DMAS * 16)
                        nc.scalar.copy(w_high[:], w_wide).then_inc(w_high_ready, 1)
                    if s in SHARED and nxt and SHARED[s][0] != "project":
                        take(n + 1, 1 - parity, *SHARED[s])

            all_pairs(sc, pair)

            def route_copy(g, par):
                sc.wait_ge(f_T, g + 1)
                at_least(sc, f_up, (g - 1) * GT)
                nc.scalar.copy(ffn_T[par], t_ps[0][:])
                nc.scalar.copy(ffn_T_high[par], t_ps[0][:]).then_inc(f_T_taken, 1)

            def route_score(g, par):
                at_least(sc, f_weight, g - 1)
                nc.scalar.activation(scores[par][:].rearrange("p t e -> p (t e)"),
                                     logits_ps, ACT.Sigmoid).then_inc(f_scores, 1)

            def expert(g, j):
                n, k = g * GT + j, j % 2
                sc.wait_ge(f_gates, n + 1)
                at_least(sc, f_silu, n - 1)
                nc.scalar.activation(sig[k][:, 0:EI], s_ps[k][:, 0:EI], ACT.Sigmoid).then_inc(f_sig, 1)

            def expert_shared(g, j):
                n, k = g * GT + j, j % 2
                nc.scalar.activation(sig[k][:, EI:EI + I], sh_ps[k][:, 0:I],
                                     ACT.Sigmoid).then_inc(f_sig_shared, 1)

            def expert_T(g, j):
                n, k = g * GT + j, j % 2
                at_least(sc, f_down, n - 1)
                sc.wait_ge(f_actT, n + 1)
                nc.scalar.copy(actT[k][:, 0:EI], t_ps[0][:])
                nc.scalar.copy(actT[k][0:I, EI:EI + P], sh_ps[k][0:I, 2 * I:2 * I + P])\
                    .then_inc(f_actT_taken, 1)

            def group(g, par, cur, prev, nxt):
                if not cur and nxt:
                    route_copy(g + 1, 1 - par)
                    sc.wait_ge(var_ready, 4)
                    nc.scalar.activation(std[:, TILES - TB:TILES], var[:, TILES - TB:TILES],
                                         ACT.Sqrt).then_inc(std_ready, 1)
                    sc.wait_ge(f_logits, 1)
                    route_score(g + 1, 1 - par)
                for j in range(GT):
                    late = before(g, j, cur, prev)
                    if late:
                        expert_T(*late)
                    if cur:
                        expert(g, j)
                    if cur:
                        sc.wait_ge(f_up, g * GT + j + 1)
                    if cur and nxt and j == 1:
                        route_score(g + 1, 1 - par)
                    if cur:
                        expert_shared(g, j)
                    if cur and nxt and j == 0:
                        route_copy(g + 1, 1 - par)
                    if prev and j == 2:
                        store(g - 1, 1 - par)

            def store(g, par):
                sc.wait_ge(f_result, g * GT + GT)
                sc.dma_start(out_t[:, bass.ds(g * GT, GT), :],
                             result[par].rearrange("p (t d) -> p t d", d=D)).then_inc(stored[par], 16)

            all_groups(sc, group)
            for done in stored:
                sc.wait_ge(done, TILES // GT // 2 * 16)

        @block.vector
        def _(dve):
            links = [0]

            def link(ins):
                links[0] += 1
                ins.then_inc(stat_link, 1)
                dve.wait_ge(stat_link, links[0])

            def spread(first, end):
                some = slice(first, end)
                me, mo = stats[:, some, 1], stats[:, some, 4]
                nc.vector.tensor_tensor(mean2[:, some], me, mo, ALU.add)
                nc.vector.tensor_tensor(diff[:, some], me, mo, ALU.subtract)
                link(nc.vector.tensor_tensor(m2[:, some], stats[:, some, 2], stats[:, some, 5], ALU.add))
                nc.vector.tensor_scalar(mean[:, some], mean2[:, some], 0.5, None, ALU.mult)
                link(nc.vector.scalar_tensor_tensor(var[:, some], diff[:, some], 0.25, diff[:, some],
                                                    ALU.mult, ALU.mult))
                link(nc.vector.scalar_tensor_tensor(var[:, some], m2[:, some], 1.0 / D, var[:, some],
                                                    ALU.mult, ALU.add))
                nc.vector.tensor_scalar(var[:, some], var[:, some], LN_EPS, None, ALU.add)\
                    .then_inc(var_ready, 1)

            def statistics(tiles):
                for t in tiles:
                    last = nc.vector.bn_stats(stats[:, t, :], stream[:, t, :])
                return last

            def normalise(b):
                for c in range(2):
                    if b > 0:
                        dve.wait_ge(normed_T, 2 * b - 1 + c)
                    for t in range(4 * c, 4 * c + 4):
                        tile = b * TB + t
                        last = nc.vector.tensor_scalar(normed[:, t, :], stream[:, tile, :],
                                                       mean[:, tile:tile + 1], rstd[:, tile:tile + 1],
                                                       ALU.subtract, ALU.mult)
                    last.then_inc(normed_ready, 1)

            def low(m, what, c, bank=m_ps[:]):
                dve.wait_ge(act_took, m * FILLS + FILL[what, c] + 1)
                high, rest = (q_high, q_low) if what == "q" else (k_high, k_low)
                nc.vector.scalar_tensor_tensor(
                    rest[:, half(c)], bank, QSCALE if what == "q" else 1.0,
                    high[:, half(c)].bitcast(F32), ALU.mult, ALU.subtract).then_inc(low_ready, 1)

            dve.wait_ge(x_loaded[0], 16)
            link(statistics(range(TB)))
            spread(0, TB)
            dve.wait_ge(std_ready, 1)
            link(nc.vector.reciprocal(rstd[:, 0:TB], std[:, 0:TB]))
            normalise(0)
            for b in range(1, B):
                dve.wait_ge(x_loaded[b], 16)
                last = statistics(range(b * TB, (b + 1) * TB))
            link(last)
            spread(TB, TILES)
            dve.wait_ge(std_ready, 2)
            link(nc.vector.reciprocal(rstd[:, TB:TILES], std[:, TB:TILES]))
            for what, c in FILL:
                if what != "v":
                    low(0, what, c, first_bank[what, c])
            for b in range(1, B):
                normalise(b)
            dve.wait_ge(consts_done, 1)

            def row_max(n, s):
                dve.wait_ge(s_ready, n * STEPS + s + 1)
                nc.vector.tensor_reduce(neg_max[:, s:s + 1], s_ps[s % 2][:], AX.X, ALU.max,
                                        negate=True).then_inc(max_ready, 1)

            def diagonal(n, s):
                dve.wait_ge(exp_done, n * STEPS + s + 1)
                blk = probs[s % P_SLOTS][:, tile_cols(s // 2)]
                nc.vector.scalar_tensor_tensor(blk, blk, 1.0, causal[:], ALU.mult, ALU.mult,
                                               accum_out=den_diag[:, s:s + 1]).then_inc(diag_done, 1)

            def denominator(n, s):
                dve.wait_ge(diag_done, n * STEPS + s + 1)
                if s // 2 > 0:
                    ins = nc.vector.tensor_scalar(den[:, s:s + 1], den_left[:, s:s + 1],
                                                  den_diag[:, s:s + 1], DEN_EPS, ALU.add, ALU.add)
                else:
                    ins = nc.vector.tensor_scalar(den[:, s:s + 1], den_diag[:, s:s + 1], DEN_EPS,
                                                  None, ALU.add)
                ins.then_inc(den_summed, 1)

            def invert(n, s):
                dve.wait_ge(den_summed, n * STEPS + s + 1)
                nc.vector.reciprocal(rden[:, s:s + 1], den[:, s:s + 1]).then_inc(rden_ready, 1)

            def take_heads(n, c):
                dve.wait_ge(pv_done, n * TT + 2 * (c + 1))
                nc.vector.tensor_copy(heads[:, half(c)], o_ps[:]).then_inc(o_taken, 1)

            def add(n, c):
                dve.wait_ge(projected, n * 2 + c + 1)
                b = n // HP if isinstance(n, int) else (n >> 3) & (B - 1)
                dst = stream[:, bass.ds(b * TB + 4 * c, 4), :]
                nc.vector.tensor_tensor(dst, m_ps[:].rearrange("p (t d) -> p t d", t=4), dst,
                                        ALU.add).then_inc(added, 1)

            def norm_group(g, par):
                at_least(dve, f_T, g - 1)
                for j in range(GT):
                    tile = g * GT + j
                    if isinstance(tile, int):
                        src = stream[:, tile, :]
                        mu, rs = mean[:, tile:tile + 1], rstd[:, tile:tile + 1]
                    else:
                        src = stream[:, bass.ds(tile, 1), :].rearrange("p a d -> p (a d)")
                        mu, rs = mean[:, bass.ds(tile, 1)], rstd[:, bass.ds(tile, 1)]
                    last = nc.vector.tensor_scalar(ffn_in[par][:, j, :], src, mu, rs,
                                                   ALU.subtract, ALU.mult)
                last.then_inc(f_normed, 1)

            def pair(n, parity, cur, prev, nxt):
                if cur and not prev:
                    dve.wait_ge(bo_added, B)
                for s in range(STEPS):
                    if prev and s - 1 in SHARED and SHARED[s - 1][0] == "project":
                        add(n - 1, SHARED[s - 1][1])
                    if cur and s == 15:
                        take_heads(n, 0)
                    if prev and s == 7:
                        take_heads(n - 1, 1)
                    if not cur and s == 3:
                        spread(0, TILES - TB)
                    if not cur and s == 8:
                        dve.wait_ge(std_ready, 3)
                        link(nc.vector.reciprocal(rstd[:, 0:TILES - TB], std[:, 0:TILES - TB]))
                        norm_group(0, 0)
                        norm_group(1, 1)
                    if cur:
                        row_max(n, s)
                    late = lagging(n, s, 2, cur, prev)
                    if late:
                        denominator(late[0], late[1])
                    late1 = lagging(n, s, 1, cur, prev)
                    if late1:
                        diagonal(late1[0], late1[1])
                    if late:
                        invert(late[0], late[1])
                    if nxt and FILL.get(SHARED.get(s - 1), FILLS) < SPLITS:
                        low(n + 1, *SHARED[s - 1])
                    if cur and not nxt and s == 13:
                        dve.wait_ge(w_high_ready, 1)
                        nc.vector.tensor_tensor(w_low[:], w_wide, w_high[:].bitcast(F32),
                                                ALU.subtract).then_inc(w_low_ready, 1)
                    if cur and not nxt and s < 3 * TB // 2:
                        statistics(range(2 * s, 2 * s + 2))

            all_pairs(dve, pair)

            dve.wait_ge(added, 2 * PAIRS)
            link(statistics(range(TILES - TB, TILES)))
            spread(TILES - TB, TILES)
            dve.wait_ge(std_ready, 4)
            link(nc.vector.reciprocal(rstd[:, TILES - TB:TILES], std[:, TILES - TB:TILES]))

            def then(g, step, ins):
                ins.then_inc(g_link, 1)
                dve.wait_ge(g_link, g * ROUTE_LINKS + step)

            def compare(g, step, values, n, tie, above, lower):
                other = values.unsqueeze(2).to_broadcast([P, GT, n, n])
                own = values.unsqueeze(3).to_broadcast([P, GT, n, n])
                nc.vector.tensor_tensor(above[:], other, own, ALU.is_gt)
                then(g, step, nc.vector.tensor_tensor(tie[:], other, own, ALU.is_equal))
                then(g, step + 1, nc.vector.tensor_tensor(
                    tie[:], tie[:], lower.unsqueeze(1).to_broadcast([P, GT, n, n]), ALU.mult))

            def rank(g, step, tie, above, rank_):
                then(g, step, nc.vector.tensor_tensor(above[:], above[:], tie[:], ALU.add))
                then(g, step + 1, nc.vector.tensor_reduce(rank_[:], above[:], AX.X, ALU.add))

            ROUTE_LINKS = 15
            by_group = biased[:].rearrange("p t (g s) -> p t g s", s=GS)

            def route_groups(g, par):
                dve.wait_ge(f_scores, g + 1)
                then(g, 1, nc.vector.tensor_tensor(
                    biased[:], scores[par][:], bias_all[:].unsqueeze(1).to_broadcast([P, GT, E]), ALU.add))
                then(g, 2, nc.vector.tensor_tensor(group_score[:], by_group[:, :, :, 0],
                                                   by_group[:, :, :, 1], ALU.add))
                compare(g, 3, group_score[:], NG, tie_g, above_g, earlier[:, 0:NG, 0:NG])
                rank(g, 5, tie_g, above_g, rank_g)

            def route_experts(g, par):
                then(g, 7, nc.vector.tensor_scalar(keep_g[:], rank_g[:], float(TOP_GROUPS), None,
                                                   ALU.is_lt))
                then(g, 8, nc.vector.tensor_tensor(
                    choice[:].rearrange("p t (g s) -> p t g s", s=GS), by_group,
                    keep_g[:].unsqueeze(3).to_broadcast([P, GT, NG, GS]), ALU.mult))
                compare(g, 9, choice[:], E, tie_e, above_e, earlier[:])

            def route_ranks(g, par):
                rank(g, 11, tie_e, above_e, rank_e)

            def route_weights(g, par):
                then(g, 13, nc.vector.scalar_tensor_tensor(picked[:], rank_e[:], float(TOPK),
                                                           scores[par][:], ALU.is_lt, ALU.mult))
                then(g, 14, nc.vector.tensor_reduce(total[:], picked[:], AX.X, ALU.add))
                then(g, 15, nc.vector.tensor_scalar(total[:], total[:], TOPK_EPS, None, ALU.add))
                nc.vector.reciprocal(rtotal[:], total[:]).then_inc(f_rtotal, 1)
                dve.wait_ge(f_rtotal, g + 1)
                at_least(dve, f_sigw, (g - 1) * GT)
                nc.vector.scalar_tensor_tensor(weight[par][:], picked[:], ROUTED_SCALE,
                                               rtotal[:].unsqueeze(2).to_broadcast([P, GT, E]),
                                               ALU.mult, ALU.mult).then_inc(f_weight, 1)

            def activate(g, j):
                n, k = g * GT + j, j % 2
                dve.wait_ge(f_sigw, n + 1)
                at_least(dve, f_actT, n - 1)
                nc.vector.tensor_tensor(act[k][:, 0:EI], s_ps[k][:, 0:EI], sig[k][:, 0:EI], ALU.mult)
                dve.wait_ge(f_sig_shared, n + 1)
                nc.vector.tensor_tensor(act[k][:, EI:EI + I], sh_ps[k][:, 0:I],
                                        sig[k][:, EI:EI + I], ALU.mult).then_inc(f_silu, 1)
                dve.wait_ge(f_silu, n + 1)
                nc.vector.tensor_tensor(act[k][:, 0:EI], s_ps[k][:, EI:2 * EI], act[k][:, 0:EI], ALU.mult)
                nc.vector.tensor_tensor(act[k][:, EI:EI + I], sh_ps[k][:, I:2 * I],
                                        act[k][:, EI:EI + I], ALU.mult).then_inc(f_act, 1)

            def finish(g, par, j):
                n = g * GT + j
                dve.wait_ge(f_down, n + 1)
                if j == 0:
                    at_least(dve, stored[par], (g >> 1) * 16)
                if isinstance(n, int):
                    src = stream[:, n, :]
                else:
                    src = stream[:, bass.ds(n, 1), :].rearrange("p a d -> p (a d)")
                nc.vector.tensor_tensor(result[par][:, tile_cols(j)], t_ps[1][:, 0:P], src, ALU.add)\
                    .then_inc(f_result, 1)

            def group(g, par, cur, prev, nxt):
                if not cur and nxt:
                    route_groups(g + 1, 1 - par)
                    route_experts(g + 1, 1 - par)
                    route_ranks(g + 1, 1 - par)
                    route_weights(g + 1, 1 - par)
                for j in range(GT):
                    if cur and j == 0 and (not isinstance(g, int) or g + 2 < TILES // GT):
                        norm_group(g + 2, par)
                    late = before(g, j, cur, prev)
                    if late:
                        finish(late[0], par if j >= LAG_DOWN else 1 - par, late[1])
                    if cur:
                        activate(g, j)
                    if cur and nxt and j == 1:
                        route_groups(g + 1, 1 - par)
                    if cur and nxt and j == 2:
                        route_experts(g + 1, 1 - par)
                    if cur and nxt and j == 3:
                        route_ranks(g + 1, 1 - par)
                        route_weights(g + 1, 1 - par)

            all_groups(dve, group)

        @block.tensor
        def _(pe):
            pe.wait_ge(consts_done, 1)
            def transpose_x(b):
                for c in range(2):
                    pe.wait_ge(normed_ready, 2 * b + c + 1)
                    if b > 0:
                        pe.wait_ge(xT_ready, 2 * b - 1 + c)
                    for j in range(4):
                        last = nc.tensor.transpose(t_ps[c][:, tile_cols(j)], normed[:, 4 * c + j, :],
                                                   ident[:])
                    last.then_inc(normed_T, 1)

            def fill(m, parity, what, c, x, bank=m_ps[:], first=False):
                if what == "v":
                    for j in range(4):
                        last = nc.tensor.matmul(bank[:, tile_cols(j)], x[:, tile_cols(4 * c + j)],
                                                wcur[parity][:, 2, :], start=True, stop=True)
                elif first:
                    last = nc.tensor.matmul(bank, wcur[parity][:, 0 if what == "q" else 1, :],
                                            x[:, half(c)], start=True, stop=True)
                else:
                    w = 0 if what == "q" else 1
                    nc.tensor.matmul(bank, wqk_high[:, w, :], x_high[:, half(c)], start=True, stop=False)
                    nc.tensor.matmul(bank, wqk_high[:, w, :], x_low[:, half(c)], start=False, stop=False)
                    last = nc.tensor.matmul(bank, wqk_low[:, w, :], x_high[:, half(c)], start=False,
                                            stop=True)
                last.then_inc(filled, 1)

            transpose_x(0)
            pe.wait_ge(first_w_loaded, 3 * 16)
            pe.wait_ge(xT_ready, 2)
            for what, c in FILL:
                fill(0, 0, what, c, xT, first_bank[what, c], True)
            for b in range(1, B):
                transpose_x(b)

            def scores_of(n, parity, s):
                t, h = s // 2, s % 2
                if s == 0:
                    pe.wait_ge(stacked, (n * STACK_DMAS + STACK_DMAS) * 16)
                at_least(pe, exp_done, n * STEPS + s - 1)
                qs = q_stack[parity][:, h, tile_cols(t)]
                for c in range(2):
                    nc.tensor.matmul(s_ps[s % 2][:, half(c)], qs, kh_stack[parity][:, h, half(c)],
                                     start=True, stop=False)
                    last = nc.tensor.matmul(s_ps[s % 2][:, half(c)], qs, kl_stack[parity][:, h, half(c)],
                                            start=False, stop=True)
                last.then_inc(s_ready, 1)

            def transposes(n, u):
                pe.wait_ge(scaled, n * STEPS + u + 1)
                t = u // 2
                for j0 in range(0, t + 1, 4):
                    g = groups_before(u) + j0 // 4
                    at_least(pe, t_taken, n * GROUPS + g - 1)
                    for j in range(j0, min(j0 + 4, t + 1)):
                        last = nc.tensor.transpose(t_ps[g % 2][:, tile_cols(j - j0)],
                                                   probs[u % P_SLOTS][:, tile_cols(j)], ident[:])
                    last.then_inc(t_ready, 1)

            def values(n, parity, two, part):
                both, second = slice(two % 2 * 2 * P, (two % 2 + 1) * 2 * P), tile_cols(two % 2 * 2 + 1)
                if two == 0:
                    blocks = [(0, tile_cols(0), tile_cols(0), True, True),
                              (0, second, tile_cols(1), True, False), (1, second, tile_cols(1), False, True)]
                else:
                    blocks = [(j, both, slice(0, 2 * P), j == 0, j == 2 * two) for j in range(2 * two + 1)]
                    blocks.insert(1, (2 * two + 1, second, tile_cols(1), False, False))
                if part == 0:
                    pe.wait_ge(t_taken, n * GROUPS + groups_before(4 * two + 4))
                    if two == 0:
                        pe.wait_ge(act_took, n * FILLS + FILLS)
                    if two % 2 == 0:
                        at_least(pe, o_taken, n * 2 + two // 2)
                    blocks = blocks[:two + 1]
                else:
                    blocks = blocks[two + 1:]
                for j, queries, cols, first, last in blocks:
                    for h in range(2):
                        ins = nc.tensor.matmul(
                            o_ps[h * DH:(h + 1) * DH, queries], v[parity][:, j, h * DH:(h + 1) * DH],
                            probsT[two % 2][h][:, j, cols], start=first, stop=last)
                if part == 1:
                    ins.then_inc(pv_done, 1)

            def project(n, c):
                pe.wait_ge(o_taken, n * 2 + c + 1)
                if isinstance(n, int):
                    w = wo[:, n % HP, :]
                else:
                    w = wo[:].rearrange("p k d -> p (k d)")[:, bass.ds((n & (HP - 1)) * D, D)]
                for j in range(4):
                    last = nc.tensor.matmul(m_ps[:, tile_cols(j)], heads[:, tile_cols(4 * c + j)],
                                            w, start=True, stop=True)
                last.then_inc(projected, 1)

            def shared(n, parity, s, cur, prev, nxt):
                what, c = SHARED[s]
                if not (prev if what == "project" else nxt):
                    return
                i = FILL.get((what, c))
                if (what, c) == ("project", 0):
                    if cur:
                        pe.wait_ge(act_took, n * FILLS + FILLS)
                    else:
                        pe.wait_ge(added, 2 * (n - 1))
                elif (what, c) == ("q", 0):
                    if prev:
                        pe.wait_ge(added, 2 * (n - 1) + 1)
                    else:
                        pe.wait_ge(act_took, FILLS)
                elif (what, c) == ("project", 1):
                    if nxt:
                        pe.wait_ge(low_ready, (n + 1) * SPLITS + SPLITS)
                    else:
                        pe.wait_ge(added, 2 * (n - 1) + 1)
                elif (what, c) == ("v", 0):
                    if prev:
                        pe.wait_ge(added, 2 * n)
                    else:
                        pe.wait_ge(low_ready, (n + 1) * SPLITS + SPLITS)
                elif (what, c) == ("v", 1):
                    pe.wait_ge(act_took, (n + 1) * FILLS + i)
                else:
                    pe.wait_ge(low_ready, (n + 1) * SPLITS + i)
                if what == "project":
                    project(n - 1, c)
                    return
                if i == 0:
                    pe.wait_ge(parts_low, (n + 1) * 3)
                fill(n + 1, 1 - parity, what, c, xcur[1 - parity])

            def pair(n, parity, cur, prev, nxt):
                for s in range(STEPS):
                    if cur:
                        scores_of(n, parity, s)
                    late = lagging(n, s, LAG_T, cur, prev)
                    if late:
                        transposes(late[0], late[1])
                    for part in range(2):
                        late = lagging(n, s, LAG_PV[part], cur, prev)
                        if late and late[1] % 4 == 3:
                            values(late[0], parity ^ late[2], late[1] // 4, part)
                    if s in SHARED:
                        shared(n, parity, s, cur, prev, nxt)

            all_pairs(pe, pair)

            def route_T(g, par):
                pe.wait_ge(f_normed, g + 1)
                at_least(pe, f_actT_taken, (g - 1) * GT - 1)
                for j in range(GT):
                    last = nc.tensor.transpose(t_ps[0][:, tile_cols(j)], ffn_in[par][:, j, :], ident[:])
                last.then_inc(f_T, 1)

            def route_logits(g, par):
                pe.wait_ge(f_T_taken, g + 1)
                for j in range(GT):
                    last = nc.tensor.matmul(logits_ps[:, j * E:(j + 1) * E], ffn_T[par][:, tile_cols(j)],
                                            wgate[:], start=True, stop=True)
                return last

            def wide(g, par, j, c):
                k, cols = j % 2, slice(c * EI, (c + 1) * EI)
                high, rest = ffn_T_high[par][:, tile_cols(j)], ffn_T_low[par][:, tile_cols(j)]
                nc.tensor.matmul(s_ps[k][:, cols], high, w_high[:, cols], start=True, stop=False)
                nc.tensor.matmul(s_ps[k][:, cols], high, w_low[:, cols], start=False, stop=False)
                return nc.tensor.matmul(s_ps[k][:, cols], rest, w_high[:, cols], start=False, stop=True)

            def gates(g, par, j):
                n = g * GT + j
                if j == 0:
                    pe.wait_ge(f_T_low, g + 1)
                at_least(pe, f_silu, n - 1)
                wide(g, par, j, 0).then_inc(f_gates, 1)

            def ups(g, par, j, route):
                n, k = g * GT + j, j % 2
                at_least(pe, f_act, n - 1)
                wide(g, par, j, 1)
                at_least(pe, f_actT_taken, n - 1)
                if route:
                    route_logits(g + 1, 1 - par)
                nc.tensor.matmul(sh_ps[k][:, 0:2 * I], ffn_T[par][:, tile_cols(j)], wshared[:],
                                 start=True, stop=True).then_inc(f_up, 1)

            def act_T(g, j, routed):
                n, k = g * GT + j, j % 2
                pe.wait_ge(f_act, n + 1)
                at_least(pe, f_actT_taken, n)
                at_least(pe, f_T_taken, routed)
                for b in range(KD):
                    nc.tensor.transpose(t_ps[0][:, tile_cols(b)], act[k][:, tile_cols(b)], ident[:])
                nc.tensor.transpose(sh_ps[k][0:I, 2 * I:2 * I + P], act[k][:, EI:EI + I], ident[:])\
                    .then_inc(f_actT, 1)

            def down(g, j):
                n, k = g * GT + j, j % 2
                pe.wait_ge(f_actT_taken, n + 1)
                at_least(pe, f_result, n)
                for b in range(KD):
                    nc.tensor.matmul(t_ps[1][:, 0:P], actT[k][:, tile_cols(b)], wd[:, b, :],
                                     start=(b == 0), stop=False)
                nc.tensor.matmul(t_ps[1][:, 0:P], actT[k][0:I, EI:EI + P], wd[0:I, KD, :],
                                 start=False, stop=True).then_inc(f_down, 1)

            def group(g, par, cur, prev, nxt):
                if not cur and nxt:
                    route_T(g + 1, 1 - par)
                    pe.wait_ge(added, 2 * PAIRS)
                    route_logits(g + 1, 1 - par).then_inc(f_logits, 1)
                    pe.wait_ge(f_scores, 1)
                for j in range(GT):
                    late = before(g, j, cur, prev)
                    if late:
                        act_T(*late, g + 2 if (nxt and j >= 1) else g + 1 if cur else g)
                    if cur:
                        gates(g, par, j)
                    if cur:
                        ups(g, par, j, nxt and j == 1)
                    if cur and nxt and j == 0:
                        route_T(g + 1, 1 - par)
                    if late:
                        down(*late)

            pe.wait_ge(w_low_ready, 1)
            all_groups(pe, group)


_INS = ["L0_attn_x", "L0_attn_Wq", "L0_attn_Wkv", "L0_attn_Wo", "L0_attn_bo", "L0_ffn_gate_w",
        "L0_ffn_correction_bias", "L0_ffn_Wg", "L0_ffn_Wu", "L0_ffn_Wd", "L0_ffn_Wg_s",
        "L0_ffn_Wu_s", "L0_ffn_Wd_s"]


def kernel(**inputs):
    import concourse.bacc as bacc
    import numpy as np
    from concourse.bass_utils import run_bass_kernel_spmd

    nc = bacc.Bacc("TRN2", target_bir_lowering=False, num_devices=1)
    arrays, args = {}, []
    for name in _INS:
        a = np.asarray(inputs[name])
        if name == "L0_ffn_gate_w":
            a = a.T
        a = np.ascontiguousarray(a)
        arrays[f"in_{name}"] = a
        args.append(nc.dram_tensor(f"in_{name}", a.shape, mybir.dt.from_np(a.dtype),
                                   kind="ExternalInput").ap())
    out = nc.dram_tensor("out", inputs["L0_attn_x"].shape, F32, kind="ExternalOutput").ap()
    build(nc, *args, out)
    r = run_bass_kernel_spmd(nc, [arrays], core_ids=[0])
    return r.results[0]["out"]
```
